# Optimizing a Trainium2 kernel written in Bass

```python
import numpy as np
import jax
import jax.numpy as jnp

def _softmax(x, axis=-1):
    return jax.nn.softmax(x, axis=axis)

def _gelu(x):
    return jax.nn.gelu(x, approximate=True)

def _silu(x):
    return jax.nn.silu(x)

def _sigmoid(x):
    return jax.nn.sigmoid(x)

def _layernorm(x, axis=-1, eps=1e-05):
    m = jnp.mean(x, axis=axis, keepdims=True)
    v = jnp.var(x, axis=axis, keepdims=True)
    return (x - m) / jnp.sqrt(v + eps)

def _scatter_add(tgt, idx, src, axis=0):
    return tgt.at[idx].add(src)

def _segment_sum(src, seg, n):
    return jax.ops.segment_sum(src, seg, n)
kernel_name = 'mk_seq_preln_d1_jaxref_r4_237fb2'

def setup_inputs(seed: int=0):
    np.random.seed(seed)
    _w = jnp.asarray

    def _L0_attn_setup():
        import jax, jax.numpy as jnp
        import numpy as np
        D_MODEL, N_HEADS, N_KV, HEAD_DIM, D_LAT = (256, 8, 2, 128, 32)
        N_REP = N_HEADS // N_KV
        B, T = (2, 512)
        key = jax.random.key(seed)
        ks = jax.random.split(key, 8)
        s = lambda fan_in: 1.0 / np.sqrt(fan_in)
        return {'x': jax.random.normal(ks[0], (B, T, D_MODEL), jnp.float32), 'wq': jax.random.normal(ks[1], (D_MODEL, N_HEADS * HEAD_DIM), jnp.float32) * s(D_MODEL), 'wk_down': jax.random.normal(ks[2], (D_MODEL, N_KV * D_LAT), jnp.float32) * s(D_MODEL), 'wv_down': jax.random.normal(ks[3], (D_MODEL, N_KV * D_LAT), jnp.float32) * s(D_MODEL), 'wk_up': jax.random.normal(ks[4], (D_LAT, HEAD_DIM), jnp.float32) * s(D_LAT), 'wv_up': jax.random.normal(ks[5], (D_LAT, HEAD_DIM), jnp.float32) * s(D_LAT), 'wo': jax.random.normal(ks[6], (N_HEADS * HEAD_DIM, D_MODEL), jnp.float32) * s(N_HEADS * HEAD_DIM)}
    _L0_attn_in = _L0_attn_setup()

    def _L0_ffn_setup():
        import jax, jax.numpy as jnp
        import numpy as np
        S, B, D, H, DH = (1024, 8, 256, 16, 64)

        def _forward(x, Wg, Wq, bq, Wkv, bkv, Wo, bo, ln_g, ln_b):
            s_len, bsz, d_model = x.shape
            n_head, _, d_head = Wq.shape
            cap = s_len // n_head
            scale = 1.0 / d_head ** 0.5
            h = jnp.transpose(x, (1, 0, 2))
            t = h
            probs = jax.nn.softmax(h @ Wg, axis=-1)
            scores = jnp.transpose(probs, (0, 2, 1))
            _, idx = jax.lax.top_k(scores, cap)
            idx = jnp.sort(idx, axis=-1)
            hg = jnp.take_along_axis(h[:, None, :, :], idx[..., None], axis=2)
            hg = jnp.transpose(hg, (1, 0, 2, 3))
            q = jnp.einsum('hbcd,hde->hbce', hg, Wq) + bq[:, None, None, :]
            kv = jnp.einsum('hbcd,hde->hbce', hg, Wkv) + bkv[:, None, None, :]
            k, v = jnp.split(kv, 2, axis=-1)
            att = jnp.einsum('hbid,hbjd->hbij', q, k) * scale
            p = jax.nn.softmax(att, axis=1)
            av = jnp.einsum('hbij,hbjd->hbid', p, v)
            ao = jnp.einsum('hbid,hde->hbie', av, Wo) + bo
            tok = jnp.transpose(idx, (1, 0, 2))
            b_ids = jnp.arange(bsz)[None, :, None]
            outs = jnp.zeros_like(t).at[b_ids, tok].add(ao)
            y = t + outs
            mu = jnp.mean(y, axis=-1, keepdims=True)
            var = jnp.var(y, axis=-1, keepdims=True)
            yn = (y - mu) * jax.lax.rsqrt(var + 1e-05) * ln_g + ln_b
            return jnp.transpose(yn, (1, 0, 2))
        key = jax.random.key(seed)
        ks = jax.random.split(key, 6)
        s = 0.02
        return {'x': jax.random.normal(ks[0], (S, B, D), jnp.float32), 'attn_mask': jnp.zeros((S, S), jnp.bool_), 'Wg': jax.random.normal(ks[1], (D, H), jnp.float32) * s, 'Wq': jax.random.normal(ks[2], (H, D, DH), jnp.float32) * s, 'bq': jnp.zeros((H, DH), jnp.float32), 'Wkv': jax.random.normal(ks[3], (H, D, 2 * DH), jnp.float32) * s, 'bkv': jnp.zeros((H, 2 * DH), jnp.float32), 'Wo': jax.random.normal(ks[4], (H, DH, D), jnp.float32) * s, 'bo': jnp.zeros((D,), jnp.float32), 'ln_g': jnp.ones((D,), jnp.float32), 'ln_b': jnp.zeros((D,), jnp.float32)}
    _L0_ffn_in = _L0_ffn_setup()
    _d = {'L0_attn_x': _L0_attn_in['x'], 'L0_attn_wq': _L0_attn_in['wq'], 'L0_attn_wk_down': _L0_attn_in['wk_down'], 'L0_attn_wv_down': _L0_attn_in['wv_down'], 'L0_attn_wk_up': _L0_attn_in['wk_up'], 'L0_attn_wv_up': _L0_attn_in['wv_up'], 'L0_attn_wo': _L0_attn_in['wo'], 'L0_ffn_attn_mask': _L0_ffn_in['attn_mask'], 'L0_ffn_Wg': _L0_ffn_in['Wg'], 'L0_ffn_Wq': _L0_ffn_in['Wq'], 'L0_ffn_bq': _L0_ffn_in['bq'], 'L0_ffn_Wkv': _L0_ffn_in['Wkv'], 'L0_ffn_bkv': _L0_ffn_in['bkv'], 'L0_ffn_Wo': _L0_ffn_in['Wo'], 'L0_ffn_bo': _L0_ffn_in['bo'], 'L0_ffn_ln_g': _L0_ffn_in['ln_g'], 'L0_ffn_ln_b': _L0_ffn_in['ln_b']}
    _x0 = _d['L0_attn_x']
    _d['L0_attn_x'] = jax.random.normal(jax.random.fold_in(jax.random.key(seed), 1), (4, 1024, 256), dtype=_x0.dtype)
    del _x0
    return _d

def reference(L0_attn_x, L0_attn_wq, L0_attn_wk_down, L0_attn_wv_down, L0_attn_wk_up, L0_attn_wv_up, L0_attn_wo, L0_ffn_attn_mask, L0_ffn_Wg, L0_ffn_Wq, L0_ffn_bq, L0_ffn_Wkv, L0_ffn_bkv, L0_ffn_Wo, L0_ffn_bo, L0_ffn_ln_g, L0_ffn_ln_b):

    def _L0_attn_ref(x, wq, wk_down, wv_down, wk_up, wv_up, wo):
        import jax, jax.numpy as jnp
        import numpy as np
        D_MODEL, N_HEADS, N_KV, HEAD_DIM, D_LAT = (256, 8, 2, 128, 32)
        N_REP = N_HEADS // N_KV
        B, T = (2, 512)
        Bq, Tq, _ = x.shape
        scale = HEAD_DIM ** (-0.5)
        q = (x @ wq).reshape(Bq, Tq, N_KV, N_REP, HEAD_DIM)
        k_lat = (x @ wk_down).reshape(Bq, Tq, N_KV, D_LAT)
        v_lat = (x @ wv_down).reshape(Bq, Tq, N_KV, D_LAT)
        k = jnp.einsum('bkhl,ld->bkhd', k_lat, wk_up)
        v = jnp.einsum('bkhl,ld->bkhd', v_lat, wv_up)
        scores = jnp.einsum('bqhrd,bkhd->bhrqk', q, k) * scale
        causal = jnp.tril(jnp.ones((Tq, Tq), dtype=bool))
        scores = jnp.where(causal, scores, jnp.finfo(scores.dtype).min)
        probs = jax.nn.softmax(scores, axis=-1)
        y = jnp.einsum('bhrqk,bkhd->bqhrd', probs, v)
        y = y.reshape(Bq, Tq, N_HEADS * HEAD_DIM)
        return y @ wo

    def _L0_ffn_ref(x, attn_mask, Wg, Wq, bq, Wkv, bkv, Wo, bo, ln_g, ln_b):
        import jax, jax.numpy as jnp
        import numpy as np
        S, B, D, H, DH = (1024, 8, 256, 16, 64)

        def _forward(x, Wg, Wq, bq, Wkv, bkv, Wo, bo, ln_g, ln_b):
            s_len, bsz, d_model = x.shape
            n_head, _, d_head = Wq.shape
            cap = s_len // n_head
            scale = 1.0 / d_head ** 0.5
            h = jnp.transpose(x, (1, 0, 2))
            t = h
            probs = jax.nn.softmax(h @ Wg, axis=-1)
            scores = jnp.transpose(probs, (0, 2, 1))
            _, idx = jax.lax.top_k(scores, cap)
            idx = jnp.sort(idx, axis=-1)
            hg = jnp.take_along_axis(h[:, None, :, :], idx[..., None], axis=2)
            hg = jnp.transpose(hg, (1, 0, 2, 3))
            q = jnp.einsum('hbcd,hde->hbce', hg, Wq) + bq[:, None, None, :]
            kv = jnp.einsum('hbcd,hde->hbce', hg, Wkv) + bkv[:, None, None, :]
            k, v = jnp.split(kv, 2, axis=-1)
            att = jnp.einsum('hbid,hbjd->hbij', q, k) * scale
            p = jax.nn.softmax(att, axis=1)
            av = jnp.einsum('hbij,hbjd->hbid', p, v)
            ao = jnp.einsum('hbid,hde->hbie', av, Wo) + bo
            tok = jnp.transpose(idx, (1, 0, 2))
            b_ids = jnp.arange(bsz)[None, :, None]
            outs = jnp.zeros_like(t).at[b_ids, tok].add(ao)
            y = t + outs
            mu = jnp.mean(y, axis=-1, keepdims=True)
            var = jnp.var(y, axis=-1, keepdims=True)
            yn = (y - mu) * jax.lax.rsqrt(var + 1e-05) * ln_g + ln_b
            return jnp.transpose(yn, (1, 0, 2))
        return _forward(x, Wg, Wq, bq, Wkv, bkv, Wo, bo, ln_g, ln_b)
    x = L0_attn_x
    x = x + _L0_attn_ref(_layernorm(x, axis=-1), L0_attn_wq, L0_attn_wk_down, L0_attn_wv_down, L0_attn_wk_up, L0_attn_wv_up, L0_attn_wo)
    x = x + _L0_ffn_ref(_layernorm(x, axis=-1), L0_ffn_attn_mask, L0_ffn_Wg, L0_ffn_Wq, L0_ffn_bq, L0_ffn_Wkv, L0_ffn_bkv, L0_ffn_Wo, L0_ffn_bo, L0_ffn_ln_g, L0_ffn_ln_b)
    return x

_drawn_inputs = setup_inputs


def setup_inputs(seed=0):
    import zlib

    import numpy as np

    out = dict(_drawn_inputs(seed))
    spreads = {'L0_ffn_bq': (0.0, 0.1),
     'L0_ffn_bkv': (0.0, 0.1),
     'L0_ffn_bo': (0.0, 0.1),
     'L0_ffn_ln_g': (1.0, 0.2),
     'L0_ffn_ln_b': (0.0, 0.1)}
    factors = {}
    for name, (base, spread) in spreads.items():
        noise = np.random.default_rng([zlib.crc32(name.encode()), seed]).standard_normal(out[name].shape)
        drawn = base * np.exp(spread * noise) if base else spread * noise
        out[name] = jnp.asarray(drawn.astype(out[name].dtype))
    for name, factor in factors.items():
        out[name] = (out[name] * factor).astype(out[name].dtype)
    return out
```

```python
from contextlib import ExitStack

import concourse.bass as bass
from concourse import mybir

B, T, D = 4, 1024, 256
NH, NKV, DH, DL = 8, 2, 128, 32
HG = NH // NKV
P = 128
TT = T // P
CH = 512
NC = T // CH
CT = CH // P
ND = D // P
KS = 3 * DL
KM = KS + 2
EPS = 1e-5
SCALE = DH ** -0.5
MASKED = -(2.0 ** 126)

TILES = [(c, kt) for c in range(NC) for kt in range(CT * (c + 1))]
NE = len(TILES)


def first_query(c, kt):
    return max(0, kt - CT * c) * P


def st_units():
    out = []
    for e, (c, kt) in enumerate(TILES):
        per = max(1, CH // (CH - first_query(c, kt)))
        per = 4 if per >= 4 else per
        out += [(e, h, per) for h in range(0, HG, per)]
    return out


ST = st_units()
NST = len(ST)
ST_END = [1 + max(n for n, u in enumerate(ST) if u[0] == e) for e in range(NE)]


def mx_units():
    out = []
    for t in range(TT):
        w = (t % CT + 1) * P
        per = HG if HG * w <= 2 * CH else 2
        out += [(t, h, per, 1, w) for h in range(0, HG, per)]
        if t >= CT:
            out += [(t, h, 2, 0, CH) for h in range(0, HG, 2)]
    return out


MX = mx_units()
NMX = len(MX)
MX_C0 = sum(u[0] < CT for u in MX)
MX_AT = [1, 1, 2, 2, 1, 2, 2, 2, 2, 2, 2, 1]
MX_FROM = [sum(MX_AT[:e]) for e in range(NE)]
assert sum(MX_AT) == NMX and NMX % 2 == 0 and NST % 2 == 0 and NE == 12

USES_START = (["wqT0", "wqT1", "wqT2", "wqT3", "upT", "wq", "wo", "xT0", "xT1", "k0", "qa0", "xT2", "xT3",
               "k1", "qa1", "v", "qb0", "qb1", "m0", "m1"])
USES_AT = {
    0: {3: ["xT0"], 4: ["xT1"], 5: ["m0", "xT2"], 6: ["sum0", "xT3"], 7: ["k0"], 8: ["qa0"], 9: ["k1"],
        10: ["v"], 11: ["qa1"], 12: ["m1", "sum1"]},
    1: {1: ["qb0"], 2: ["qb1"], 5: ["m0"], 6: ["sum0"], 8: ["f0"], 9: ["f1"], 12: ["m1", "sum1", "f2", "f3"]},
}
USES_AT_LAST = {
    0: {5: ["m0"], 6: ["sum0"], 12: ["m1", "sum1"]},
    1: {6: ["sum0"], 8: ["f0"], 9: ["f1"], 12: ["sum1", "f2", "f3"]},
}


def program(nc, x_d, wq_d, wkd_d, wvd_d, wku_d, wvu_d, wo_d, lng_d, lnb_d, out_d):
    F, R, BF = mybir.dt.float32, mybir.dt.float32r, mybir.dt.bfloat16
    ACT, ALU, AX = mybir.ActivationFunctionType, mybir.AluOpType, mybir.AxisListType

    with ExitStack() as ctx:
        def sb(name, shape, dtype=F):
            return ctx.enter_context(nc.sbuf_tensor(name, shape, dtype))

        def ps(name, shape, dtype=F):
            return ctx.enter_context(nc.psum_tensor(name, shape, dtype))

        def sem(name):
            return ctx.enter_context(nc.semaphore(name))

        ident = sb("ident", [P, P])
        identb = sb("identb", [P, P], BF)
        maskb = sb("maskb", [P, P], BF)
        ones = sb("ones", [P, DL])
        minus_half = sb("minus_half", [P, TT])
        lng = sb("lng", [P, D])
        lnb = sb("lnb", [P, D])
        wqk = sb("wqk", [P, ND, NH * DL])
        wkd = sb("wkd", [P, ND, NKV * DL])
        wvd = sb("wvd", [P, ND, NKV * DL])
        wvo = sb("wvo", [P, NKV, D])
        upT = sb("upT", [P, 2, DL])
        up = sb("up", [DL, 2, DH])
        x = sb("x", [P, B, TT, D])
        xn = sb("xn", [P, TT, D])
        xnT = sb("xnT", [P, ND, T])
        q_hi = [sb(f"q_hi{g}", [P, T], R) for g in range(NKV)]
        q_lo = [sb(f"q_lo{g}", [P, T], R) for g in range(NKV)]
        k_hi = sb("k_hi", [NKV * DL, T], R)
        k_lo = sb("k_lo", [NKV * DL, T], R)
        v_both = sb("v_both", [P, TT, NKV * DL])
        qs = [sb(f"qs{g}", [KM, NC, HG, CH], R) for g in range(NKV)]
        ks = [sb(f"ks{g}", [KM, T], R) for g in range(NKV)]
        v = [sb(f"v{g}", [P, TT, DL]) for g in range(NKV)]
        pr = sb("pr", [P, 8, HG, CH])
        u_raw = sb("u_raw", [P, CH])
        rsum = sb("rsum", [P, CH])
        uT = [sb(f"uT{g}", [P, T]) for g in range(NKV)]
        mx_part = sb("mx_part", [P, NC, 2, HG, CT])
        mx_all = sb("mx_all", [P, HG, CT])
        mx_split = sb("mx_split", [P, 2, HG, CT], R)
        mx_row = sb("mx_row", [2 * HG * CT, P], R)
        st1 = sb("st1", [P, TT, 6])
        mv1 = sb("mv1", [P, TT, 2])
        var1 = sb("var1", [P, TT])
        rstd1 = sb("rstd1", [P, TT])
        st2 = sb("st2", [P, CT, 6])
        mv2 = sb("mv2", [P, CT, 2])
        var2 = sb("var2", [P, CT])
        rstd2 = sb("rstd2", [P, CT])
        x1b = xn[:, 0:CT, :]
        x1 = xn[:, CT:TT, :]
        y = sb("y", [P, CT, D])
        wq_in = pr[:, 0, :, :].rearrange("p a b -> p (a b)").rearrange("p (c n) -> p c n", c=ND)
        wo_in = pr[:, 1, :, :].rearrange("p a b -> p (a b)").rearrange("p (h n) -> p h n", h=NH)
        wqT = pr[:, 2, :, :].rearrange("p a b -> p (a b)").rearrange("p (h n) -> p h n", h=NH)

        mx_ps = [ps(f"mx_ps{i}", [P, 2 * CH]) for i in range(2)]
        st_ps = [ps(f"st_ps{i}", [P, CH]) for i in range(2)]
        u_ps = ps("u_ps", [P, CH])
        sh_ps = ps("sh_ps", [P, CH])

        weights_in = sem("weights_in")
        x0_in = sem("x0_in")
        x_in = sem("x_in")
        const_step = sem("const_step")
        consts_ready = sem("consts_ready")
        sh_full = sem("sh_full")
        sh_read = sem("sh_read")
        hi_ready = sem("hi_ready")
        mx_full = sem("mx_full")
        mx_free = sem("mx_free")
        mx_step = sem("mx_step")
        max_ready = sem("max_ready")
        rows_in = sem("rows_in")
        st_full = sem("st_full")
        exp_done = sem("exp_done")
        diag_done = sem("diag_done")
        pair_done = sem("pair_done")
        pv_done = sem("pv_done")
        u_read = sem("u_read")
        rsum_ready = sem("rsum_ready")
        u_ready = sem("u_ready")
        v_ready = sem("v_ready")
        qstack_in = [[sem(f"qstack_in{g}{c}") for c in range(NC)] for g in range(NKV)]
        kstack_in = [[sem(f"kstack_in{g}{c}") for c in range(NC)] for g in range(NKV)]
        ln_step = sem("ln_step")
        var_ready = sem("var_ready")
        rstd_ready = sem("rstd_ready")
        xn_ready = sem("xn_ready")
        x1_ready = sem("x1_ready")
        x1b_ready = sem("x1b_ready")
        y_ready = sem("y_ready")
        out_done = sem("out_done")
        carrier = sem("carrier")

        def uses(g, last):
            return (USES_AT_LAST if last else USES_AT)[g]

        def flat(table):
            return [name for e in range(NE + 1) for name in table.get(e, [])]

        def wait_apart(eng, *waits):
            for s, v in waits:
                eng.wait_ge(s, v)
                eng.sem_inc(carrier, 1)

        PV_AHEAD, PAIRS_AHEAD, RSUMS_AHEAD, U_AHEAD, Y_AHEAD = 3, 2, 2, 1, 1

        def pv_count(w, tiles):
            return w * NE + (PV_AHEAD + tiles)

        def pair_count(w, pairs):
            return w * (NE // 2) + (PAIRS_AHEAD + pairs)

        def rsum_count(w, chunks):
            return w * NC + (RSUMS_AHEAD + chunks)

        def u_count(w, chunks):
            return w * NC + (U_AHEAD + chunks)

        def y_count(b, chunks):
            return b * NC + (Y_AHEAD + chunks)

        PER_BATCH = sum(len(flat(USES_AT[g])) for g in range(NKV))

        def use_no(b, g, last, name):
            before = len(flat(uses(0, last))) if g else 0
            return b * PER_BATCH + (len(USES_START) + before + flat(uses(g, last)).index(name))

        def uses_before(b, g, last):
            return b * PER_BATCH + (len(USES_START) + (len(flat(uses(0, last))) if g else 0))

        block = ctx.enter_context(nc.Block())

        @block.sync
        def _(sp):
            sp.dma_start(x[:, 0, :, :], x_d[0].rearrange("(t p) d -> p t d", p=P)).then_inc(x0_in, 16)
            sp.dma_start(wq_in, wq_d.rearrange("(c p) n -> p c n", p=P)).then_inc(weights_in, 16)
            sp.dma_start(up[:, 0, :], wku_d).then_inc(weights_in, 16)
            sp.dma_start(up[:, 1, :], wvu_d).then_inc(weights_in, 16)
            sp.dma_start(wkd[:, :, :], wkd_d.rearrange("(c p) n -> p c n", p=P)).then_inc(weights_in, 16)
            sp.dma_start(wvd[:, :, :], wvd_d.rearrange("(c p) n -> p c n", p=P)).then_inc(weights_in, 16)
            sp.dma_start(wo_in, wo_d.rearrange("(h p) n -> p h n", p=P)).then_inc(weights_in, 16)
            sp.dma_start(lng[:, :], lng_d[None, :].to_broadcast([P, D])).then_inc(weights_in, 16)
            sp.dma_start(lnb[:, :], lnb_d[None, :].to_broadcast([P, D])).then_inc(weights_in, 16)
            for b in range(1, B):
                sp.dma_start(x[:, b, :, :], x_d[b].rearrange("(t p) d -> p t d", p=P)).then_inc(x_in, 16)

            def stack_q(g, c):
                s = slice(c * CH, (c + 1) * CH)
                for piece, src in enumerate((q_hi[g], q_hi[g], q_lo[g])):
                    for h in range(HG):
                        sp.dma_start(qs[g][piece * DL:(piece + 1) * DL, c, h, :].bitcast(F),
                                     src[h * DL:(h + 1) * DL, s].bitcast(F)).then_inc(qstack_in[g][c], 16)

            def stack_k(g, c):
                s = slice(c * CH, (c + 1) * CH)
                for piece, src in enumerate((k_hi, k_lo, k_hi)):
                    sp.dma_start(ks[g][piece * DL:(piece + 1) * DL, s].bitcast(F),
                                 src[g * DL:(g + 1) * DL, s].bitcast(F)).then_inc(kstack_in[g][c], 16)

            def after_use(name):
                sp.wait_ge(sh_read, USES_START.index(name) + 1)

            after_use("k0")
            stack_k(0, 0)
            after_use("qa0")
            stack_q(0, 0)
            after_use("k1")
            stack_k(0, 1)
            after_use("qa1")
            stack_q(0, 1)
            stack_k(1, 0)
            stack_k(1, 1)
            after_use("qb0")
            stack_q(1, 0)
            after_use("qb1")
            stack_q(1, 1)

            def batch(b):
                w = b * 2
                wait_apart(sp, (st_full, w * NST + ST_END[7]),
                           (sh_read, use_no(b, 0, False, "k0") + 1))
                stack_k(0, 0)
                wait_apart(sp, (sh_read, use_no(b, 0, False, "qa0") + 1))
                stack_q(0, 0)
                wait_apart(sp, (st_full, w * NST + NST),
                           (sh_read, use_no(b, 0, False, "k1") + 1))
                stack_k(0, 1)
                wait_apart(sp, (sh_read, use_no(b, 0, False, "qa1") + 1))
                stack_q(0, 1)
                wait_apart(sp, (st_full, w * NST + (NST + ST_END[3])),
                           (sh_read, use_no(b, 1, False, "qb0") + 1))
                stack_q(1, 0)
                wait_apart(sp, (st_full, w * NST + (NST + ST_END[7])))
                stack_k(1, 0)
                wait_apart(sp, (st_full, w * NST + 2 * NST))
                stack_k(1, 1)
                wait_apart(sp, (sh_read, use_no(b, 1, False, "qb1") + 1))
                stack_q(1, 1)
                put(b, 0)
                put(b, 1)

            def put(b, c):
                wait_apart(sp, (y_ready, y_count(b, c + 1)))
                sp.dma_start(out_d.rearrange("b (c t p) d -> b c p t d", c=NC, p=P)[b, c], y[:, :, :]
                             ).then_inc(out_done, 16)

            with sp.Fori(0, B - 1) as b:
                batch(b)
            put(B - 1, 0)
            put(B - 1, 1)
            sp.wait_ge(out_done, 16 * y_count(B, 0))

        @block.tensor
        def _(pe):
            def shared(n):
                if not (isinstance(n, int) and n == 0):
                    pe.wait_ge(sh_read, n)

            def st(w, g, n):
                e, h0, nh = ST[n]
                c, kt = TILES[e]
                off = first_query(c, kt)
                width = CH - off
                if n == 0 or ST[n - 1][0] != e:
                    if kt == 0:
                        pe.wait_ge(rows_in, w * 64 + 32 * (c + 1))
                if not (isinstance(w, int) and w == 0 and n < 2):
                    pe.wait_ge(exp_done, w * NST + (n - 1))
                nc.tensor.matmul(st_ps[n % 2][:, 0:nh * width], ks[g][0:KM, kt * P:(kt + 1) * P],
                                 qs[g][0:KM, c, h0:h0 + nh, off:CH], start=True, stop=True).then_inc(st_full, 1)

            def mx(w, bb, g, n):
                t, h0, nh, own, width = MX[n]
                if n == 0:
                    pe.wait_ge(qstack_in[g][0], (bb + 1) * 16 * 3 * HG)
                    pe.wait_ge(kstack_in[g][0], (bb + 1) * 16 * 3)
                if n == MX_C0:
                    pe.wait_ge(qstack_in[g][1], (bb + 1) * 16 * 3 * HG)
                    pe.wait_ge(kstack_in[g][1], (bb + 1) * 16 * 3)
                if not (isinstance(w, int) and w == 0 and n < 2):
                    pe.wait_ge(mx_free, w * NMX + (n - 1))
                pitch = 2 * CH // nh if width * nh > CH else width
                k0 = (t // CT) * CH if own else 0
                bank = mx_ps[n % 2]
                for i in range(nh):
                    last = nc.tensor.matmul(bank[:, i * pitch:i * pitch + width],
                                            qs[g][0:KS, t // CT, h0 + i, t % CT * P:(t % CT + 1) * P],
                                            ks[g][0:KS, k0:k0 + width], start=True, stop=not own)
                    if own:
                        last = nc.tensor.matmul(bank[:, i * pitch + width - P:i * pitch + width],
                                                identb[:, :], maskb[:, :], start=False, stop=True)
                last.then_inc(mx_full, 1)

            def pv(w, g, e):
                c, kt = TILES[e]
                off = first_query(c, kt)
                slot = e // 2 if e % 2 == 0 else 6 + (e // 2) % 2
                if e == 0:
                    pe.wait_ge(v_ready, w + 1)
                if kt == 0 and not (isinstance(w, int) and w == 0 and c == 0):
                    pe.wait_ge(u_read, u_count(w, c))
                if kt >= CT * c:
                    pe.wait_ge(diag_done, w * TT + (kt + 1))
                else:
                    pe.wait_ge(exp_done, w * NST + ST_END[e])
                for h in range(HG):
                    last = nc.tensor.matmul(u_ps[h * DL:(h + 1) * DL, off:CH], v[g][:, kt, :],
                                            pr[:, slot, h, off:CH], start=kt == 0, stop=kt == CT * (c + 1) - 1)
                last.then_inc(pv_done, 1)

            def sums(w, c):
                pairs = [e for e in range(0, NE, 2) if TILES[e][0] == c]
                for e in pairs:
                    off = first_query(*TILES[e])
                    pe.wait_ge(pair_done, pair_count(w, e // 2 + 1))
                    for h in range(HG):
                        last = nc.tensor.matmul(sh_ps[h * DL:(h + 1) * DL, off:CH], ones[:, :],
                                                pr[:, e // 2, h, off:CH], start=e == pairs[0], stop=e == pairs[-1])
                return last

            def fill(name, n, w, wn, b, nb, g):
                shared(n)
                c = int(name[-1]) if name[-1].isdigit() else 0
                kind = name.rstrip("0123456789")
                if kind == "xT":
                    pe.wait_ge(xn_ready, nb + 1)
                    for i in range(2):
                        for d in range(ND):
                            j = 2 * i + d
                            last = nc.tensor.transpose(sh_ps[:, j * P:(j + 1) * P],
                                                       xn[:, 2 * c + i, d * P:(d + 1) * P], ident[:, :])
                elif kind == "k":
                    for d in range(ND):
                        last = nc.tensor.matmul(sh_ps[0:NKV * DL, :], wkd[:, d, :],
                                                xnT[:, d, c * CH:(c + 1) * CH], start=d == 0, stop=d == ND - 1)
                elif kind in ("qa", "qb"):
                    for d in range(ND):
                        gq = 0 if kind == "qa" else 1
                        last = nc.tensor.matmul(sh_ps[:, :], wqk[:, d, gq * P:(gq + 1) * P],
                                                xnT[:, d, c * CH:(c + 1) * CH], start=d == 0, stop=d == ND - 1)
                elif kind == "v":
                    for t in range(TT):
                        for d in range(ND):
                            last = nc.tensor.matmul(sh_ps[:, t * NKV * DL:(t + 1) * NKV * DL],
                                                    xnT[:, d, t * P:(t + 1) * P], wvd[:, d, :],
                                                    start=d == 0, stop=d == ND - 1)
                elif kind == "m":
                    pe.wait_ge(max_ready, wn * NC + (c + 1))
                    last = nc.tensor.transpose(sh_ps[0:2 * HG * CT, 0:P],
                                               mx_split[:, :, :, :].rearrange("p a h t -> p (a h t)").bitcast(F),
                                               ident[:, :])
                elif kind == "sum":
                    last = sums(w, c)
                else:
                    if c == 0:
                        pe.wait_ge(u_ready, u_count(w, 1))
                    if c == 2:
                        pe.wait_ge(u_ready, u_count(w, 2))
                    for i in range(2):
                        t = 2 * c + i
                        for gg in range(NKV):
                            last = nc.tensor.matmul(sh_ps[:, i * D:(i + 1) * D], uT[gg][:, t * P:(t + 1) * P],
                                                    wvo[:, gg, :], start=gg == 0, stop=gg == NKV - 1)
                last.then_inc(sh_full, 1)

            pe.sem_inc(pv_done, PV_AHEAD)
            pe.wait_ge(weights_in, 8 * 16)
            pe.wait_ge(consts_ready, 2)
            for n in range(4):
                shared(n)
                for i in range(2):
                    for d in range(ND):
                        j = 2 * i + d
                        last = nc.tensor.transpose(sh_ps[:, j * P:(j + 1) * P],
                                                   wq_in[:, d, (2 * n + i) * DH:(2 * n + i + 1) * DH], ident[:, :])
                last.then_inc(sh_full, 1)
            shared(4)
            for i in range(2):
                last = nc.tensor.transpose(sh_ps[:, i * DL:(i + 1) * DL], up[:, i, :], ident[0:DL, 0:DL])
            last.then_inc(sh_full, 1)
            shared(5)
            for d in range(ND):
                for h in range(NH):
                    last = nc.tensor.matmul(sh_ps[:, d * D + h * DL:d * D + (h + 1) * DL],
                                            wqT[:, h, d * P:(d + 1) * P], upT[:, 0, :], start=True, stop=True)
            last.then_inc(sh_full, 1)
            shared(6)
            for h in range(NH):
                gg, j = h // HG, h % HG
                last = nc.tensor.matmul(sh_ps[j * DL:(j + 1) * DL, gg * D:(gg + 1) * D], upT[:, 1, :],
                                        wo_in[:, h, :], start=True, stop=True)
            last.then_inc(sh_full, 1)
            for n, name in enumerate(USES_START[7:], 7):
                if name == "m0":
                    for i in range(MX_C0):
                        mx(0, 0, 0, i)
                if name == "m1":
                    for i in range(MX_C0, NMX):
                        mx(0, 0, 0, i)
                fill(name, n, 0, 0, 0, 0, 0)
            for n in range(ST_END[0]):
                st(0, 0, n)

            def batch(b, last):
                for g in range(NKV):
                    w = b * 2 + g
                    wn = b * 2 + (g + 1)
                    no_m = last and g == 1
                    at = uses(g, last)
                    for e in range(NE):
                        units = list(range(ST_END[e - 1], ST_END[e])) if e else []
                        beside = [] if no_m else list(range(MX_FROM[e], MX_FROM[e] + MX_AT[e]))
                        if units:
                            st(w, g, units.pop(0))
                        if beside:
                            mx(wn, b + g, 1 - g, beside.pop(0))
                        if units:
                            st(w, g, units.pop(0))
                        if e:
                            pv(w, g, e - 1)
                        if units:
                            st(w, g, units.pop(0))
                        if beside:
                            mx(wn, b + g, 1 - g, beside.pop(0))
                        if units:
                            st(w, g, units.pop(0))
                        for name in at.get(e, []):
                            fill(name, use_no(b, g, last, name), w, wn, b, b + 1, g)
                    if not no_m:
                        for n in range(ST_END[0]):
                            st(wn, 1 - g, n)
                    pv(w, g, NE - 1)
                    for name in at.get(NE, []):
                        fill(name, use_no(b, g, last, name), w, wn, b, b + 1, g)

            with pe.Fori(0, B - 1) as b:
                batch(b, False)
            batch(B - 1, True)

        @block.scalar
        def _(act):
            def exps(w, e):
                c, kt = TILES[e]
                off = first_query(c, kt)
                width = CH - off
                slot = e // 2 if e % 2 == 0 else 6 + (e // 2) % 2
                first = isinstance(w, int) and w == 0
                if e % 2 == 0:
                    if not first:
                        act.wait_ge(rsum_ready, rsum_count(w, c - 1))
                elif not (first and e < 4):
                    act.wait_ge(pv_done, pv_count(w, e - 3))
                    act.wait_ge(pair_done, pair_count(w, e // 2 - 1))
                for n in range(ST_END[e - 1] if e else 0, ST_END[e]):
                    _, h0, nh = ST[n]
                    act.wait_ge(st_full, w * NST + (n + 1))
                    nc.scalar.activation(pr[:, slot, h0:h0 + nh, off:CH],
                                         st_ps[n % 2][:, 0:nh * width].rearrange("p (h q) -> p h q", h=nh),
                                         ACT.Exp, scale=SCALE).then_inc(exp_done, 1)

            def copy_u(w, c):
                act.wait_ge(pv_done, pv_count(w, CT if c == 0 else NE))
                if not (isinstance(w, int) and w == 0 and c == 0):
                    act.wait_ge(u_ready, u_count(w, c))
                nc.scalar.activation(u_raw[:, :], u_ps[:, :], ACT.Copy).then_inc(u_read, 1)

            def read(name, n, wn, nb, g):
                c = int(name[-1]) if name[-1].isdigit() else 0
                kind = name.rstrip("0123456789")
                if kind in ("sum", "f"):
                    return
                act.wait_ge(sh_full, n + 1)
                if kind == "xT":
                    dst = xnT[:, :, 2 * c * P:2 * (c + 1) * P].rearrange("p d (i q) -> p i d q", i=2)
                    nc.scalar.activation(dst, sh_ps[:, :].rearrange("p (i d q) -> p i d q", i=2, d=ND), ACT.Copy
                                         ).then_inc(sh_read, 1)
                elif kind == "k":
                    for gg in range(NKV):
                        if not (isinstance(nb, int) and nb == 0):
                            act.wait_ge(kstack_in[gg][c], nb * 16 * 3)
                    nc.scalar.activation(k_hi[:, c * CH:(c + 1) * CH], sh_ps[0:NKV * DL, :], ACT.Copy
                                         ).then_inc(hi_ready, 1)
                elif kind in ("qa", "qb"):
                    gq = 0 if kind == "qa" else 1
                    if not (isinstance(nb, int) and nb == 0):
                        act.wait_ge(qstack_in[gq][c], nb * 16 * 3 * HG)
                    nc.scalar.activation(q_hi[gq][:, c * CH:(c + 1) * CH], sh_ps[:, :], ACT.Copy
                                         ).then_inc(hi_ready, 1)
                elif kind == "v":
                    if not (isinstance(nb, int) and nb == 0):
                        act.wait_ge(v_ready, nb * 2)
                    nc.scalar.activation(v_both[:, :, :].rearrange("p t n -> p (t n)"), sh_ps[:, :], ACT.Copy
                                         ).then_inc(sh_read, 1)
                else:
                    if not (isinstance(wn, int) and wn == 0 and c == 0):
                        act.wait_ge(rows_in, wn * 64 + 32 * c)
                    nc.scalar.activation(mx_row[:, :], sh_ps[0:2 * HG * CT, 0:P], ACT.Copy).then_inc(sh_read, 1)
                    act.wait_ge(sh_read, n + 1)
                    for part in range(2):
                        act.dma_start(qs[g][KS + part:KS + part + 1, c, :, :].rearrange("p h q -> p (h q)")
                                      .rearrange("p (r q) -> p r q", q=P).bitcast(F),
                                      mx_row[part * HG * CT:(part + 1) * HG * CT, :].bitcast(F)
                                      ).then_inc(rows_in, 16)

            for n in range(4):
                act.wait_ge(sh_full, n + 1)
                nc.scalar.activation(wqT[:, 2 * n:2 * n + 2, :].rearrange("p h n -> p (h n)"), sh_ps[:, :], ACT.Copy
                                     ).then_inc(sh_read, 1)
            act.wait_ge(sh_full, 5)
            nc.scalar.activation(upT[:, :, :].rearrange("p a l -> p (a l)"), sh_ps[:, 0:2 * DL], ACT.Copy
                                 ).then_inc(sh_read, 1)
            act.wait_ge(sh_full, 6)
            nc.scalar.activation(wqk[:, :, :].rearrange("p d n -> p (d n)"), sh_ps[:, :], ACT.Copy
                                 ).then_inc(sh_read, 1)
            act.wait_ge(sh_full, 7)
            nc.scalar.activation(wvo[:, :, :].rearrange("p g n -> p (g n)"), sh_ps[:, :], ACT.Copy
                                 ).then_inc(sh_read, 1)
            for n, name in enumerate(USES_START[7:], 7):
                read(name, n, 0, 0, 0)
            exps(0, 0)

            def batch(b, last):
                for g in range(NKV):
                    w = b * 2 + g
                    wn = b * 2 + (g + 1)
                    at = uses(g, last)
                    for e in range(NE):
                        if e:
                            exps(w, e)
                        if e == CT:
                            copy_u(w, 0)
                        for name in at.get(e, []):
                            read(name, use_no(b, g, last, name), wn, b + 1, 1 - g)
                    if not (last and g == 1):
                        exps(wn, 0)
                    copy_u(w, 1)
                    for name in at.get(NE, []):
                        read(name, use_no(b, g, last, name), wn, b + 1, 1 - g)

            with act.Fori(0, B - 1) as b:
                batch(b, False)
            batch(B - 1, True)

        @block.vector
        def _(dve):
            def maxima(w, n):
                t, h0, nh, own, width = MX[n]
                pitch = 2 * CH // nh if width * nh > CH else width
                dve.wait_ge(mx_full, w * NMX + (n + 1))
                nc.vector.tensor_reduce(mx_part[:, t // CT, own, h0:h0 + nh, t % CT],
                                        mx_ps[n % 2][:, 0:nh * pitch].rearrange("p (h k) -> p h k", h=nh)[:, :, 0:width],
                                        AX.X, ALU.max).then_inc(mx_free, 1)

            def split_max(w, c, uses_done):
                dve.wait_ge(mx_free, w * NMX + (NMX if c else MX_C0))
                dve.wait_ge(sh_full, uses_done)
                m = mx_part[:, 0, 1, :, :]
                if c:
                    nc.vector.tensor_tensor(mx_all[:, :, :], mx_part[:, 1, 0, :, :], mx_part[:, 1, 1, :, :], ALU.max
                                            ).then_inc(mx_step, 1)
                    dve.wait_ge(mx_step, w * 3 + 2)
                    m = mx_all[:, :, :]
                nc.vector.tensor_scalar(mx_split[:, 0, :, :], m, -1.0, None, ALU.mult).then_inc(mx_step, 1)
                dve.wait_ge(mx_step, w * 3 + (3 if c else 1))
                nc.vector.scalar_tensor_tensor(out=mx_split[:, 1, :, :], in0=m, scalar=-1.0,
                                               in1=mx_split[:, 0, :, :].bitcast(F), op0=ALU.mult, op1=ALU.subtract
                                               ).then_inc(max_ready, 1)

            def norm1_stats(bb, half, steps):
                for t in range(half * CT, (half + 1) * CT):
                    last = nc.vector.bn_stats(st1[:, t, :], x[:, bb, t, :])
                if half:
                    last.then_inc(ln_step, 1)
                    wait_apart(dve, (ln_step, steps + 1))
                    for t in range(TT):
                        last = nc.vector.bn_aggr(mv1[:, t, :], st1[:, t, :])
                    last.then_inc(ln_step, 1)
                    dve.wait_ge(ln_step, steps + 2)
                    nc.vector.tensor_scalar(var1[:, :], mv1[:, :, 1], EPS, None, ALU.add).then_inc(var_ready, 1)

            def norm1_apply(bb, powers):
                dve.wait_ge(rstd_ready, powers)
                for t in range(TT):
                    last = nc.vector.tensor_scalar(xn[:, t, :], x[:, bb, t, :], mv1[:, t, 0:1], rstd1[:, t:t + 1],
                                                   ALU.subtract, ALU.mult)
                last.then_inc(xn_ready, 1)

            def divide(w, g, c, n):
                dve.wait_ge(sh_full, n + 1)
                nc.vector.tensor_copy(rsum[:, :], sh_ps[:, :]).then_inc(sh_read, 1)
                dve.wait_ge(sh_read, n + 1)
                nc.vector.reciprocal(rsum[:, :], rsum[:, :]).then_inc(rsum_ready, 1)
                dve.wait_ge(rsum_ready, rsum_count(w, c + 1))
                dve.wait_ge(u_read, u_count(w, c + 1))
                nc.vector.tensor_tensor(uT[g][:, c * CH:(c + 1) * CH], u_raw[:, :], rsum[:, :], ALU.mult
                                        ).then_inc(u_ready, 1)

            def residual(b, j, n):
                dve.wait_ge(sh_full, n + 1)
                i = 2 * (j % 2)
                nc.vector.tensor_tensor(x1[:, i:i + 2, :], sh_ps[:, :].rearrange("p (i d) -> p i d", i=2),
                                        x[:, b, 2 * j:2 * j + 2, :], ALU.add).then_inc(sh_read, 1)
                dve.wait_ge(sh_read, n + 1)
                for t in range(i, i + 2):
                    last = nc.vector.bn_stats(st2[:, t, :], x1[:, t, :])
                return last

            def norm2_stats(b, c, last, steps):
                last.then_inc(ln_step, 1)
                wait_apart(dve, (ln_step, steps + 1))
                for t in range(CT):
                    last = nc.vector.bn_aggr(mv2[:, t, :], st2[:, t, :])
                last.then_inc(ln_step, 1)
                dve.wait_ge(ln_step, steps + 2)
                nc.vector.tensor_scalar(var2[:, :], mv2[:, :, 1], 1.0 + EPS, EPS * EPS, ALU.mult, ALU.add
                                        ).then_inc(var_ready, 1)

            def norm2_apply(b, c, powers, steps):
                if not (isinstance(b, int) and b == 0 and c == 0):
                    dve.wait_ge(out_done, y_count(b, c) * 16)
                for t in range(CT):
                    last = nc.vector.scalar_tensor_tensor(out=y[:, t, :], in0=x1[:, t, :], scalar=mv2[:, t, 0:1],
                                                          in1=lng[:, :], op0=ALU.subtract, op1=ALU.mult)
                last.then_inc(ln_step, 1)
                dve.wait_ge(ln_step, steps + 3)
                dve.wait_ge(rstd_ready, powers)
                dve.wait_ge(x1b_ready, b * NC + (c + 1))
                for t in range(CT):
                    last = nc.vector.scalar_tensor_tensor(out=y[:, t, :], in0=y[:, t, :], scalar=rstd2[:, t:t + 1],
                                                          in1=x1b[:, t, :], op0=ALU.mult, op1=ALU.add)
                last.then_inc(y_ready, 1)

            def low(name, n, nb):
                c = int(name[-1])
                kind = name.rstrip("0123456789")
                order = ["k0", "qa0", "k1", "qa1", "qb0", "qb1"]
                dve.wait_ge(sh_full, n + 1)
                dve.wait_ge(hi_ready, nb * len(order) + (order.index(name) + 1))
                s = slice(c * CH, (c + 1) * CH)
                if kind == "k":
                    nc.vector.tensor_tensor(k_lo[:, s], sh_ps[0:NKV * DL, :], k_hi[:, s].bitcast(F), ALU.subtract
                                            ).then_inc(sh_read, 1)
                else:
                    gq = 0 if kind == "qa" else 1
                    nc.vector.tensor_tensor(q_lo[gq][:, s], sh_ps[:, :], q_hi[gq][:, s].bitcast(F), ALU.subtract
                                            ).then_inc(sh_read, 1)

            dve.sem_inc(rsum_ready, RSUMS_AHEAD)
            dve.sem_inc(u_ready, U_AHEAD)
            dve.sem_inc(u_read, U_AHEAD)
            for g in range(NKV):
                nc.vector.memset(ks[g][KS:KM, :].bitcast(F), 1.0)
            nc.vector.memset(ones[:, :], 1.0)
            nc.vector.memset(minus_half[:, :], -0.5).then_inc(consts_ready, 1)
            dve.wait_ge(x0_in, 16)
            norm1_stats(0, 0, 0)
            norm1_stats(0, 1, 0)
            norm1_apply(0, 1)
            for n, name in enumerate(USES_START):
                if name[0] in "kq":
                    low(name, n, 0)
                if name == "m0":
                    for i in range(MX_C0):
                        maxima(0, i)
                    split_max(0, 0, n)
                if name == "m1":
                    for i in range(MX_C0, NMX):
                        maxima(0, i)
                    split_max(0, 1, n)
            dve.wait_ge(x_in, 16 * (B - 1))

            def batch(b, last):
                steps = b * 8 + 2
                powers = b * 3 + 1
                for g in range(NKV):
                    w = b * 2 + g
                    wn = b * 2 + (g + 1)
                    no_m = last and g == 1
                    at = uses(g, last)
                    stats = None
                    for e in range(NE + 1):
                        if e < NE and not no_m:
                            for n in range(MX_FROM[e], MX_FROM[e] + MX_AT[e]):
                                maxima(wn, n)
                            if MX_FROM[e] < MX_C0 <= MX_FROM[e] + MX_AT[e]:
                                split_max(wn, 0, uses_before(b, g, last))
                            if e == NE - 1:
                                split_max(wn, 1, use_no(b, g, last, "m0") + 1)
                        if g == 0 and not last:
                            if e < 2:
                                norm1_stats(b + 1, e, steps)
                            if e == 2:
                                norm1_apply(b + 1, powers + 1)
                        for name in at.get(e, []):
                            n = use_no(b, g, last, name)
                            if name[0] in "kq":
                                low(name, n, b + 1)
                            if name[:3] == "sum":
                                divide(w, g, int(name[3]), n)
                            if name[0] == "f":
                                c = int(name[1]) // 2
                                stats = residual(b, int(name[1]), n)
                                if name in ("f1", "f3"):
                                    s = steps + ((0 if last else 2) + 3 * c)
                                    p = powers + ((0 if last else 1) + c + 1)
                                    norm2_stats(b, c, stats, s)
                                    norm2_apply(b, c, p, s)

            with dve.Fori(0, B - 1) as b:
                batch(b, False)
            batch(B - 1, True)

        @block.gpsimd
        def _(pool):
            pool.sem_inc(pair_done, PAIRS_AHEAD)
            pool.sem_inc(y_ready, Y_AHEAD)
            pool.sem_inc(out_done, 16 * Y_AHEAD)
            nc.gpsimd.memset(ident[:, :], 0.0).then_inc(const_step, 1)
            nc.gpsimd.memset(maskb[:, :], 0.0).then_inc(const_step, 1)
            pool.wait_ge(const_step, 2)
            nc.gpsimd.affine_select(out=ident[:, :], in_=ident[:, :], compare_op=ALU.not_equal, fill=1.0, base=0,
                                    pattern=[[-1, P]], channel_multiplier=1).then_inc(const_step, 1)
            nc.gpsimd.affine_select(out=maskb[:, :], in_=maskb[:, :], compare_op=ALU.is_ge, fill=MASKED, base=0,
                                    pattern=[[-1, P]], channel_multiplier=1).then_inc(const_step, 1)
            pool.wait_ge(const_step, 4)
            nc.gpsimd.tensor_copy(identb[:, :], ident[:, :]).then_inc(consts_ready, 1)

            def rsqrt(out, in_, n, count):
                pool.wait_ge(var_ready, count)
                nc.gpsimd.tensor_tensor(out, in_, minus_half[:, 0:n], ALU.pow).then_inc(rstd_ready, 1)

            def diagonal(w, e):
                c, kt = TILES[e]
                off = first_query(c, kt)
                slot = e // 2 if e % 2 == 0 else 6 + (e // 2) % 2
                wait_apart(pool, (exp_done, w * NST + ST_END[e]))
                blk = pr[:, slot, :, off:off + P]
                nc.gpsimd.affine_select(out=blk, in_=blk, compare_op=ALU.is_ge, fill=0.0, base=0,
                                        pattern=[[0, HG], [1, P]], channel_multiplier=-1).then_inc(diag_done, 1)

            def pair(w, e):
                c, kt = TILES[e]
                off = first_query(c, kt)
                pool.wait_ge(pv_done, pv_count(w, e))
                if kt >= CT * c:
                    pool.wait_ge(diag_done, w * TT + (kt + 1))
                else:
                    pool.wait_ge(exp_done, w * NST + ST_END[e])
                even = pr[:, e // 2, :, off:CH]
                nc.gpsimd.tensor_tensor(even, even, pr[:, 6 + (e // 2) % 2, :, off:CH], ALU.add).then_inc(pair_done, 1)

            def take_v(g):
                nc.gpsimd.tensor_copy(v[g][:, :, :], v_both[:, :, g * DL:(g + 1) * DL]).then_inc(v_ready, 1)

            def add_bias(b, c, reads, written):
                pool.wait_ge(sh_read, reads)
                pool.wait_ge(y_ready, written)
                nc.gpsimd.tensor_tensor(x1b[:, :, :], x1[:, :, :], lnb[:, None, :].to_broadcast([P, CT, D]), ALU.add
                                        ).then_inc(x1b_ready, 1)

            pool.wait_ge(consts_ready, 2)
            pool.wait_ge(weights_in, 16 * 8)
            rsqrt(rstd1[:, :], var1[:, :], TT, 1)
            pool.wait_ge(sh_read, USES_START.index("v") + 1)
            take_v(0)
            take_v(1)
            diagonal(0, 0)

            def batch(b, last):
                powers = b * 3 + 1
                for g in range(NKV):
                    w = b * 2 + g
                    wn = b * 2 + (g + 1)
                    for e in range(1, NE):
                        if g == 0 and e == 2 and not last:
                            rsqrt(rstd1[:, :], var1[:, :], TT, powers + 1)
                        c, kt = TILES[e]
                        if kt >= CT * c:
                            diagonal(w, e)
                        if e % 2:
                            pair(w, e)
                        if g == 1 and e == 9:
                            rsqrt(rstd2[:, :], var2[:, :], CT, powers + (1 if last else 2))
                            add_bias(b, 0, use_no(b, 1, last, "f1") + 1, y_count(b, 0))
                    if not (last and g == 1):
                        diagonal(wn, 0)
                    if not last:
                        wait_apart(pool, (pv_done, pv_count(w, NE)),
                                   (sh_read, use_no(b, 0, last, "v") + 1))
                        take_v(g)
                    if g == 1:
                        rsqrt(rstd2[:, :], var2[:, :], CT, powers + (2 if last else 3))
                        add_bias(b, 1, use_no(b, 1, last, "f3") + 1, y_count(b, 1))

            with pool.Fori(0, B - 1) as b:
                batch(b, False)
            batch(B - 1, True)


def kernel(L0_attn_x, L0_attn_wq, L0_attn_wk_down, L0_attn_wv_down, L0_attn_wk_up, L0_attn_wv_up, L0_attn_wo,
           L0_ffn_ln_g, L0_ffn_ln_b, **unused):
    import numpy as np
    from concourse import bacc
    from concourse.bass_utils import run_bass_kernel_spmd

    nc = bacc.Bacc("TRN2", target_bir_lowering=False, num_devices=1)
    given = {"x": L0_attn_x, "wq": L0_attn_wq, "wk_down": L0_attn_wk_down, "wv_down": L0_attn_wv_down,
             "wk_up": L0_attn_wk_up, "wv_up": L0_attn_wv_up, "wo": L0_attn_wo,
             "ln_g": L0_ffn_ln_g, "ln_b": L0_ffn_ln_b}
    arrays, args = {}, []
    for name, a in given.items():
        a = np.ascontiguousarray(a)
        arrays[f"in_{name}"] = a
        args.append(nc.dram_tensor(f"in_{name}", a.shape, mybir.dt.from_np(a.dtype), kind="ExternalInput").ap())
    out = nc.dram_tensor("out_y", (B, T, D), mybir.dt.float32, kind="ExternalOutput").ap()
    program(nc, *args, out)
    result = run_bass_kernel_spmd(nc, [arrays], core_ids=[0])
    return result.results[0]["out_y"]
```

```python
from contextlib import ExitStack

import concourse.bass as bass
from concourse import mybir

B, T, D = 4, 1024, 256
NH, NKV, DH, DL = 8, 2, 128, 32
HG = NH // NKV
P = 128
TT = T // P
CH = 512
NC = T // CH
CT = CH // P
ND = D // P
KS = 3 * DL
KM = KS + 2
EPS = 1e-5
SCALE = DH ** -0.5
MASKED = -(2.0 ** 126)

TILES = [(c, kt) for c in range(NC) for kt in range(CT * (c + 1))]
NE = len(TILES)


def first_query(c, kt):
    return max(0, kt - CT * c) * P


def st_units():
    out = []
    for e, (c, kt) in enumerate(TILES):
        per = max(1, CH // (CH - first_query(c, kt)))
        per = 4 if per >= 4 else per
        out += [(e, h, per) for h in range(0, HG, per)]
    return out


ST = st_units()
NST = len(ST)
ST_END = [1 + max(n for n, u in enumerate(ST) if u[0] == e) for e in range(NE)]


def mx_units():
    out = []
    for t in range(TT):
        w = (t % CT + 1) * P
        per = HG if HG * w <= 2 * CH else 2
        out += [(t, h, per, 1, w) for h in range(0, HG, per)]
        if t >= CT:
            out += [(t, h, 2, 0, CH) for h in range(0, HG, 2)]
    return out


MX = mx_units()
NMX = len(MX)
MX_C0 = sum(u[0] < CT for u in MX)
MX_AT = [1, 1, 1, 1, 1, 1, 2, 2, 2, 2, 3, 3]
MX_FROM = [sum(MX_AT[:e]) for e in range(NE)]
assert sum(MX_AT) == NMX and NMX % 2 == 0 and NST % 2 == 0 and NE == 12

USES_START = ["wqT0", "wqT1", "wqT2", "wqT3", "upT", "wq", "wo", "xT0", "xT1", "k0", "qa0", "xT2", "xT3",
              "k1", "qa1", "v", "qb0", "qb1", "m0"]
FIRST, MID, LAST = 0, 1, 2
WINDOW0 = [[], ["m1", "sum1"], ["sT1"], ["rT1", "xT0"], ["f2", "xT1"], ["f3", "m0"], ["sum0", "xT2"],
           ["sT0", "xT3"], ["rT0", "k0"], ["qa0", "k1"], ["v"], ["qa1"]]
WINDOW1 = [[], ["m1", "sum1"], ["sT1"], ["rT1", "qb0"], ["qb1"], ["m0"], ["sum0"],
           ["sT0"], ["rT0"], ["f0"], ["f1"], []]


def without(window, *names):
    return [[u for u in uses if u not in names] for uses in window]


USES_AT = {
    FIRST: [without(WINDOW0, "sum1", "sT1", "rT1", "f2", "f3"), WINDOW1],
    MID: [WINDOW0, WINDOW1],
    LAST: [without(WINDOW0, "xT0", "xT1", "xT2", "xT3", "k0", "k1", "qa0", "qa1", "v"),
           without(WINDOW1, "qb0", "qb1", "m0")],
}
USES_END = ["sum1", "sT1", "rT1", "f2", "f3"]
APPLY_AT = [8, 11]


def program(nc, x_d, wq_d, wkd_d, wvd_d, wku_d, wvu_d, wo_d, lng_d, lnb_d, out_d):
    F, R, BF = mybir.dt.float32, mybir.dt.float32r, mybir.dt.bfloat16
    ACT, ALU, AX = mybir.ActivationFunctionType, mybir.AluOpType, mybir.AxisListType

    with ExitStack() as ctx:
        def sb(name, shape, dtype=F):
            return ctx.enter_context(nc.sbuf_tensor(name, shape, dtype))

        def ps(name, shape, dtype=F):
            return ctx.enter_context(nc.psum_tensor(name, shape, dtype))

        def sem(name):
            return ctx.enter_context(nc.semaphore(name))

        ident = sb("ident", [P, P])
        identb = sb("identb", [P, P], BF)
        maskb = sb("maskb", [P, P], BF)
        ones = sb("ones", [P, DL])
        minus_half = sb("minus_half", [P, TT])
        lng = sb("lng", [P, D])
        lnb = sb("lnb", [P, D])
        wqk = sb("wqk", [P, ND, NH * DL])
        wkd = sb("wkd", [P, ND, NKV * DL])
        wvd = sb("wvd", [P, ND, NKV * DL])
        wvo = sb("wvo", [P, NKV, D])
        upT = sb("upT", [P, 2, DL])
        up = sb("up", [DL, 2, DH])
        x = sb("x", [P, B, TT, D])
        xn = sb("xn", [P, TT, D])
        xnT = sb("xnT", [P, ND, T])
        q_hi = sb("q_hi", [P, T], R)
        q_lo = sb("q_lo", [P, T], R)
        k_hi = sb("k_hi", [NKV * DL, T], R)
        k_lo = sb("k_lo", [NKV * DL, T], R)
        v_both = sb("v_both", [P, TT, NKV * DL])
        qs = [sb(f"qs{g}", [KM, NC, HG, CH], R) for g in range(NKV)]
        ks = [sb(f"ks{g}", [KM, T], R) for g in range(NKV)]
        v = [sb(f"v{g}", [P, TT, DL]) for g in range(NKV)]
        pr = sb("pr", [P, 8, HG, CH])
        u_raw = sb("u_raw", [P, CH])
        s_raw = sb("s_raw", [P, CH])
        r_q = sb("r_q", [P, CT, HG])
        r_wide = sb("r_wide", [P, CT, HG, DL])
        uT = [sb(f"uT{g}", [P, T]) for g in range(NKV)]
        mx_part = sb("mx_part", [P, NC, 2, HG, CT])
        mx_all = sb("mx_all", [P, HG, CT])
        mx_split = sb("mx_split", [P, 2, HG, CT], R)
        mx_row = sb("mx_row", [2 * HG * CT, P], R)
        st1 = sb("st1", [P, TT, 6])
        mv1 = sb("mv1", [P, TT, 2])
        var1 = sb("var1", [P, TT])
        rstd1 = sb("rstd1", [P, TT])
        st2 = sb("st2", [P, CT, 6])
        mv2 = sb("mv2", [P, CT, 2])
        var2 = sb("var2", [P, CT])
        rstd2 = sb("rstd2", [P, CT])
        x1b = sb("x1b", [P, CT, D])
        y = sb("y", [P, CT, D])
        wq_in = pr[:, 0, :, :].rearrange("p a b -> p (a b)").rearrange("p (c n) -> p c n", c=ND)
        wo_in = pr[:, 1, :, :].rearrange("p a b -> p (a b)").rearrange("p (h n) -> p h n", h=NH)
        wqT = pr[:, 2, :, :].rearrange("p a b -> p (a b)").rearrange("p (h n) -> p h n", h=NH)

        mx_ps = [ps(f"mx_ps{i}", [P, 2 * CH]) for i in range(2)]
        st_ps = [ps(f"st_ps{i}", [P, CH]) for i in range(2)]
        u_ps = ps("u_ps", [P, CH])
        sh_ps = ps("sh_ps", [P, CH])

        weights_in = sem("weights_in")
        x0_in = sem("x0_in")
        x_in = sem("x_in")
        const_step = sem("const_step")
        consts_ready = sem("consts_ready")
        sh_full = sem("sh_full")
        sh_read = sem("sh_read")
        hi_ready = sem("hi_ready")
        mx_full = sem("mx_full")
        mx_free = sem("mx_free")
        mx_step = sem("mx_step")
        max_ready = sem("max_ready")
        rows_in = sem("rows_in")
        st_full = sem("st_full")
        exp_done = sem("exp_done")
        diag_done = sem("diag_done")
        pair_done = sem("pair_done")
        pv_done = sem("pv_done")
        u_read = sem("u_read")
        wide_ready = sem("wide_ready")
        u_ready = sem("u_ready")
        v_ready = sem("v_ready")
        qstack_in = [[sem(f"qstack_in{g}{c}") for c in range(NC)] for g in range(NKV)]
        kstack_in = [[sem(f"kstack_in{g}{c}") for c in range(NC)] for g in range(NKV)]
        ln_step = sem("ln_step")
        var_ready = sem("var_ready")
        rstd_ready = sem("rstd_ready")
        xn_ready = sem("xn_ready")
        x1_ready = sem("x1_ready")
        x1b_ready = sem("x1b_ready")
        y_ready = sem("y_ready")
        out_done = sem("out_done")
        carrier = sem("carrier")

        def flat(table):
            return [name for e in range(NE) for name in table[e]]

        def wait_apart(eng, *waits):
            for s, v in waits:
                eng.wait_ge(s, v)
                eng.sem_inc(carrier, 1)

        PV_AHEAD, PAIRS_AHEAD, U_AHEAD, Y_AHEAD = 3, 2, 1, 1

        def pv_count(w, tiles):
            return w * NE + (PV_AHEAD + tiles)

        def pair_count(w, pairs):
            return w * (NE // 2) + (PAIRS_AHEAD + pairs)

        def u_count(w, chunks):
            return w * NC + (U_AHEAD + chunks)

        def y_count(b, chunks):
            return b * NC + (Y_AHEAD + chunks)

        def uses_of(kind):
            return sum(len(flat(USES_AT[kind][g])) for g in range(NKV))

        def uses_before(b):
            if isinstance(b, int) and b == 0:
                return len(USES_START)
            return (b - 1) * uses_of(MID) + (len(USES_START) + uses_of(FIRST))

        def use_no(b, g, kind, name):
            before = len(flat(USES_AT[kind][0])) if g else 0
            return uses_before(b) + (before + flat(USES_AT[kind][g]).index(name))

        USES_ALL = uses_before(B - 1) + uses_of(LAST)

        def sum0_before(b, g, kind):
            if g:
                return use_no(b, 0, kind, "sum0")
            names = flat(USES_AT[MID][1])
            return uses_before(b) - (len(names) - names.index("sum0"))

        block = ctx.enter_context(nc.Block())

        @block.sync
        def _(sp):
            sp.dma_start(x[:, 0, :, :], x_d[0].rearrange("(t p) d -> p t d", p=P)).then_inc(x0_in, 16)
            sp.dma_start(wq_in, wq_d.rearrange("(c p) n -> p c n", p=P)).then_inc(weights_in, 16)
            sp.dma_start(up[:, 0, :], wku_d).then_inc(weights_in, 16)
            sp.dma_start(up[:, 1, :], wvu_d).then_inc(weights_in, 16)
            sp.dma_start(wkd[:, :, :], wkd_d.rearrange("(c p) n -> p c n", p=P)).then_inc(weights_in, 16)
            sp.dma_start(wvd[:, :, :], wvd_d.rearrange("(c p) n -> p c n", p=P)).then_inc(weights_in, 16)
            sp.dma_start(wo_in, wo_d.rearrange("(h p) n -> p h n", p=P)).then_inc(weights_in, 16)
            sp.dma_start(lng[:, :], lng_d[None, :].to_broadcast([P, D])).then_inc(weights_in, 16)
            sp.dma_start(lnb[:, :], lnb_d[None, :].to_broadcast([P, D])).then_inc(weights_in, 16)
            for b in range(1, B):
                sp.dma_start(x[:, b, :, :], x_d[b].rearrange("(t p) d -> p t d", p=P)).then_inc(x_in, 16)

            def stack_q(g, c):
                s = slice(c * CH, (c + 1) * CH)
                for piece, src in enumerate((q_hi, q_hi, q_lo)):
                    sp.dma_start(qs[g][piece * DL:(piece + 1) * DL, c, :, :].bitcast(F), src[:, s].bitcast(F)
                                 ).then_inc(qstack_in[g][c], 16)

            def stack_k(g, c):
                s = slice(c * CH, (c + 1) * CH)
                for piece, src in enumerate((k_hi, k_lo, k_hi)):
                    sp.dma_start(ks[g][piece * DL:(piece + 1) * DL, s].bitcast(F),
                                 src[g * DL:(g + 1) * DL, s].bitcast(F)).then_inc(kstack_in[g][c], 16)

            def after_use(name):
                sp.wait_ge(sh_read, USES_START.index(name) + 1)

            after_use("k0")
            stack_k(0, 0)
            after_use("qa0")
            stack_q(0, 0)
            after_use("k1")
            stack_k(0, 1)
            after_use("qa1")
            stack_q(0, 1)
            stack_k(1, 0)
            stack_k(1, 1)
            after_use("qb0")
            stack_q(1, 0)
            after_use("qb1")
            stack_q(1, 1)

            def batch(b, kind):
                w = b * 2
                if kind != FIRST:
                    put(b - 1, 1)
                wait_apart(sp, (st_full, w * NST + ST_END[7]),
                           (sh_read, use_no(b, 0, kind, "k0") + 1))
                stack_k(0, 0)
                wait_apart(sp, (sh_read, use_no(b, 0, kind, "qa0") + 1))
                stack_q(0, 0)
                wait_apart(sp, (st_full, w * NST + NST),
                           (sh_read, use_no(b, 0, kind, "k1") + 1))
                stack_k(0, 1)
                wait_apart(sp, (sh_read, use_no(b, 0, kind, "qa1") + 1))
                stack_q(0, 1)
                wait_apart(sp, (st_full, w * NST + (NST + ST_END[3])),
                           (sh_read, use_no(b, 1, kind, "qb0") + 1))
                stack_q(1, 0)
                wait_apart(sp, (st_full, w * NST + (NST + ST_END[7])))
                stack_k(1, 0)
                put(b, 0)
                wait_apart(sp, (st_full, w * NST + 2 * NST))
                stack_k(1, 1)
                wait_apart(sp, (sh_read, use_no(b, 1, kind, "qb1") + 1))
                stack_q(1, 1)

            def put(b, c):
                wait_apart(sp, (y_ready, y_count(b, c + 1)))
                sp.dma_start(out_d.rearrange("b (c t p) d -> b c p t d", c=NC, p=P)[b, c], y[:, :, :]
                             ).then_inc(out_done, 16)

            batch(0, FIRST)
            with sp.Fori(1, B - 1) as b:
                batch(b, MID)
            put(B - 2, 1)
            put(B - 1, 0)
            put(B - 1, 1)
            sp.wait_ge(out_done, 16 * y_count(B, 0))

        @block.tensor
        def _(pe):
            def shared(n):
                if not (isinstance(n, int) and n == 0):
                    pe.wait_ge(sh_read, n)

            def st(w, g, n):
                e, h0, nh = ST[n]
                c, kt = TILES[e]
                off = first_query(c, kt)
                width = CH - off
                if n == 0 or ST[n - 1][0] != e:
                    if kt == 0:
                        pe.wait_ge(rows_in, w * 64 + 32 * (c + 1))
                if not (isinstance(w, int) and w == 0 and n < 2):
                    pe.wait_ge(exp_done, w * NST + (n - 1))
                nc.tensor.matmul(st_ps[n % 2][:, 0:nh * width], ks[g][0:KM, kt * P:(kt + 1) * P],
                                 qs[g][0:KM, c, h0:h0 + nh, off:CH], start=True, stop=True).then_inc(st_full, 1)

            def mx(w, bb, g, n):
                t, h0, nh, own, width = MX[n]
                if n == 0:
                    pe.wait_ge(qstack_in[g][0], (bb + 1) * 16 * 3)
                    pe.wait_ge(kstack_in[g][0], (bb + 1) * 16 * 3)
                if n == MX_C0:
                    pe.wait_ge(qstack_in[g][1], (bb + 1) * 16 * 3)
                    pe.wait_ge(kstack_in[g][1], (bb + 1) * 16 * 3)
                if not (isinstance(w, int) and w == 0 and n < 2):
                    pe.wait_ge(mx_free, w * NMX + (n - 1))
                pitch = 2 * CH // nh if width * nh > CH else width
                k0 = (t // CT) * CH if own else 0
                bank = mx_ps[n % 2]
                for i in range(nh):
                    last = nc.tensor.matmul(bank[:, i * pitch:i * pitch + width],
                                            qs[g][0:KS, t // CT, h0 + i, t % CT * P:(t % CT + 1) * P],
                                            ks[g][0:KS, k0:k0 + width], start=True, stop=not own)
                    if own:
                        last = nc.tensor.matmul(bank[:, i * pitch + width - P:i * pitch + width],
                                                identb[:, :], maskb[:, :], start=False, stop=True)
                last.then_inc(mx_full, 1)

            def pv(w, g, e):
                c, kt = TILES[e]
                off = first_query(c, kt)
                slot = e // 2 if e % 2 == 0 else 6 + (e // 2) % 2
                if e == 0:
                    pe.wait_ge(v_ready, w + 1)
                if kt == 0 and not (isinstance(w, int) and w == 0 and c == 0):
                    pe.wait_ge(u_read, u_count(w, c))
                if kt >= CT * c:
                    pe.wait_ge(diag_done, w * TT + (kt + 1))
                else:
                    pe.wait_ge(exp_done, w * NST + ST_END[e])
                for h in range(HG):
                    last = nc.tensor.matmul(u_ps[h * DL:(h + 1) * DL, off:CH], v[g][:, kt, :],
                                            pr[:, slot, h, off:CH], start=kt == 0, stop=kt == CT * (c + 1) - 1)
                last.then_inc(pv_done, 1)

            def sums(w, c):
                pairs = [e for e in range(0, NE, 2) if TILES[e][0] == c]
                for e in pairs:
                    off = first_query(*TILES[e])
                    pe.wait_ge(pair_done, pair_count(w, e // 2 + 1))
                    for h in range(HG):
                        last = nc.tensor.matmul(sh_ps[h * DL:(h + 1) * DL, off:CH], ones[:, :],
                                                pr[:, e // 2, h, off:CH], start=e == pairs[0], stop=e == pairs[-1])
                return last

            def fill(name, n, w, wn, nb):
                shared(n)
                c = int(name[-1]) if name[-1].isdigit() else 0
                kind = name.rstrip("0123456789")
                if kind == "xT":
                    pe.wait_ge(xn_ready, nb + 1)
                    for i in range(2):
                        for d in range(ND):
                            j = 2 * i + d
                            last = nc.tensor.transpose(sh_ps[:, j * P:(j + 1) * P],
                                                       xn[:, 2 * c + i, d * P:(d + 1) * P], ident[:, :])
                elif kind == "k":
                    for d in range(ND):
                        last = nc.tensor.matmul(sh_ps[0:NKV * DL, :], wkd[:, d, :],
                                                xnT[:, d, c * CH:(c + 1) * CH], start=d == 0, stop=d == ND - 1)
                elif kind in ("qa", "qb"):
                    for d in range(ND):
                        gq = 0 if kind == "qa" else 1
                        last = nc.tensor.matmul(sh_ps[:, :], wqk[:, d, gq * P:(gq + 1) * P],
                                                xnT[:, d, c * CH:(c + 1) * CH], start=d == 0, stop=d == ND - 1)
                elif kind == "v":
                    for t in range(TT):
                        for d in range(ND):
                            last = nc.tensor.matmul(sh_ps[:, t * NKV * DL:(t + 1) * NKV * DL],
                                                    xnT[:, d, t * P:(t + 1) * P], wvd[:, d, :],
                                                    start=d == 0, stop=d == ND - 1)
                elif kind == "m":
                    pe.wait_ge(max_ready, wn * NC + 1 if c == 0 else w * NC + 2)
                    last = nc.tensor.transpose(sh_ps[0:2 * HG * CT, 0:P],
                                               mx_split[:, :, :, :].rearrange("p a h t -> p (a h t)").bitcast(F),
                                               ident[:, :])
                elif kind == "sum":
                    last = sums(w - c, c)
                elif kind == "sT":
                    for t in range(CT):
                        last = nc.tensor.transpose(sh_ps[:, t * P:(t + 1) * P], s_raw[:, t * P:(t + 1) * P],
                                                   ident[:, :])
                elif kind == "rT":
                    pe.wait_ge(wide_ready, w * NC + (1 - c))
                    for t in range(CT):
                        last = nc.tensor.transpose(sh_ps[:, t * P:(t + 1) * P],
                                                   r_wide[:, t, :, :].rearrange("p h l -> p (h l)"), ident[:, :])
                else:
                    if c == 0:
                        pe.wait_ge(u_ready, u_count(w, 1))
                    if c == 2:
                        pe.wait_ge(u_ready, u_count(w - 1, 2))
                    for i in range(2):
                        t = 2 * c + i
                        for gg in range(NKV):
                            last = nc.tensor.matmul(sh_ps[:, i * D:(i + 1) * D], uT[gg][:, t * P:(t + 1) * P],
                                                    wvo[:, gg, :], start=gg == 0, stop=gg == NKV - 1)
                last.then_inc(sh_full, 1)

            pe.sem_inc(pv_done, PV_AHEAD)
            pe.wait_ge(weights_in, 8 * 16)
            pe.wait_ge(consts_ready, 2)
            for n in range(4):
                shared(n)
                for i in range(2):
                    for d in range(ND):
                        j = 2 * i + d
                        last = nc.tensor.transpose(sh_ps[:, j * P:(j + 1) * P],
                                                   wq_in[:, d, (2 * n + i) * DH:(2 * n + i + 1) * DH], ident[:, :])
                last.then_inc(sh_full, 1)
            shared(4)
            for i in range(2):
                last = nc.tensor.transpose(sh_ps[:, i * DL:(i + 1) * DL], up[:, i, :], ident[0:DL, 0:DL])
            last.then_inc(sh_full, 1)
            shared(5)
            for d in range(ND):
                for h in range(NH):
                    last = nc.tensor.matmul(sh_ps[:, d * D + h * DL:d * D + (h + 1) * DL],
                                            wqT[:, h, d * P:(d + 1) * P], upT[:, 0, :], start=True, stop=True)
            last.then_inc(sh_full, 1)
            shared(6)
            for h in range(NH):
                gg, j = h // HG, h % HG
                last = nc.tensor.matmul(sh_ps[j * DL:(j + 1) * DL, gg * D:(gg + 1) * D], upT[:, 1, :],
                                        wo_in[:, h, :], start=True, stop=True)
            last.then_inc(sh_full, 1)
            for n, name in enumerate(USES_START[7:], 7):
                if name == "m0":
                    for i in range(MX_C0):
                        mx(0, 0, 0, i)
                fill(name, n, 0, 0, 0)
            for n in range(ST_END[0]):
                st(0, 0, n)
            for i in range(MX_C0, NMX):
                mx(0, 0, 0, i)

            def batch(b, kind):
                for g in range(NKV):
                    w = b * 2 + g
                    wn = b * 2 + (g + 1)
                    no_m = kind == LAST and g == 1
                    for e in range(NE):
                        units = list(range(ST_END[e - 1], ST_END[e])) if e else []
                        beside = [] if no_m else list(range(MX_FROM[e], MX_FROM[e] + MX_AT[e]))
                        names = list(USES_AT[kind][g][e])
                        for part in range(4):
                            if units:
                                st(w, g, units.pop(0))
                            if part == 1 and names:
                                name = names.pop(0)
                                fill(name, use_no(b, g, kind, name), w, wn, b + 1)
                            if part == 1 and e:
                                pv(w, g, e - 1)
                            if part != 1 and beside:
                                mx(wn, b + g, 1 - g, beside.pop(0))
                            if part == 3 and names:
                                name = names.pop(0)
                                fill(name, use_no(b, g, kind, name), w, wn, b + 1)
                    if not no_m:
                        for n in range(ST_END[0]):
                            st(wn, 1 - g, n)
                    pv(w, g, NE - 1)

            batch(0, FIRST)
            with pe.Fori(1, B - 1) as b:
                batch(b, MID)
            batch(B - 1, LAST)
            for i, name in enumerate(USES_END):
                fill(name, USES_ALL + i, 2 * B, 0, 0)

        @block.scalar
        def _(act):
            def exps(w, e, sum_before, between=None):
                c, kt = TILES[e]
                off = first_query(c, kt)
                width = CH - off
                slot = e // 2 if e % 2 == 0 else 6 + (e // 2) % 2
                first = isinstance(w, int) and w == 0
                if e % 2 == 0:
                    if not first:
                        act.wait_ge(sh_full, sum_before + 1)
                elif not (first and e < 4):
                    act.wait_ge(pv_done, pv_count(w, e - 3))
                    act.wait_ge(pair_done, pair_count(w, e // 2 - 1))
                n0 = ST_END[e - 1] if e else 0
                for n in range(n0, ST_END[e]):
                    _, h0, nh = ST[n]
                    if n == n0 + 2 and between:
                        between()
                    act.wait_ge(st_full, w * NST + (n + 1))
                    nc.scalar.activation(pr[:, slot, h0:h0 + nh, off:CH],
                                         st_ps[n % 2][:, 0:nh * width].rearrange("p (h q) -> p h q", h=nh),
                                         ACT.Exp, scale=SCALE).then_inc(exp_done, 1)

            def copy_u(w, c):
                act.wait_ge(pv_done, pv_count(w, CT if c == 0 else NE))
                if not (isinstance(w, int) and w == 0 and c == 0):
                    act.wait_ge(u_ready, u_count(w, c))
                nc.scalar.activation(u_raw[:, :], u_ps[:, :], ACT.Copy).then_inc(u_read, 1)

            def read(name, n, w, g, nb):
                c = int(name[-1]) if name[-1].isdigit() else 0
                kind = name.rstrip("0123456789")
                if kind in ("sT", "rT", "f"):
                    return
                act.wait_ge(sh_full, n + 1)
                if kind == "xT":
                    dst = xnT[:, :, 2 * c * P:2 * (c + 1) * P].rearrange("p d (i q) -> p i d q", i=2)
                    nc.scalar.activation(dst, sh_ps[:, :].rearrange("p (i d q) -> p i d q", i=2, d=ND), ACT.Copy
                                         ).then_inc(sh_read, 1)
                elif kind == "k":
                    for gg in range(NKV):
                        if not (isinstance(nb, int) and nb == 0):
                            act.wait_ge(kstack_in[gg][c], nb * 16 * 3)
                    nc.scalar.activation(k_hi[:, c * CH:(c + 1) * CH], sh_ps[0:NKV * DL, :], ACT.Copy
                                         ).then_inc(hi_ready, 1)
                elif kind in ("qa", "qb"):
                    if kind == "qb":
                        act.wait_ge(qstack_in[0][c], (nb + 1) * 16 * 3)
                    elif not (isinstance(nb, int) and nb == 0):
                        act.wait_ge(qstack_in[1][c], nb * 16 * 3)
                    nc.scalar.activation(q_hi[:, c * CH:(c + 1) * CH], sh_ps[:, :], ACT.Copy
                                         ).then_inc(hi_ready, 1)
                elif kind == "sum":
                    nc.scalar.activation(s_raw[:, :], sh_ps[:, :], ACT.Copy).then_inc(sh_read, 1)
                elif kind == "v":
                    if not (isinstance(nb, int) and nb == 0):
                        act.wait_ge(v_ready, nb * 2)
                    nc.scalar.activation(v_both[:, :, :].rearrange("p t n -> p (t n)"), sh_ps[:, :], ACT.Copy
                                         ).then_inc(sh_read, 1)
                else:
                    wm, gm = (w + 1, 1 - g) if c == 0 else (w, g)
                    if not (isinstance(wm, int) and wm == 0 and c == 0):
                        act.wait_ge(rows_in, wm * 64 + 32 * c)
                    nc.scalar.activation(mx_row[:, :], sh_ps[0:2 * HG * CT, 0:P], ACT.Copy).then_inc(sh_read, 1)
                    act.wait_ge(sh_read, n + 1)
                    for part in range(2):
                        act.dma_start(qs[gm][KS + part:KS + part + 1, c, :, :].rearrange("p h q -> p (h q)")
                                      .rearrange("p (r q) -> p r q", q=P).bitcast(F),
                                      mx_row[part * HG * CT:(part + 1) * HG * CT, :].bitcast(F)
                                      ).then_inc(rows_in, 16)

            for n in range(4):
                act.wait_ge(sh_full, n + 1)
                nc.scalar.activation(wqT[:, 2 * n:2 * n + 2, :].rearrange("p h n -> p (h n)"), sh_ps[:, :], ACT.Copy
                                     ).then_inc(sh_read, 1)
            act.wait_ge(sh_full, 5)
            nc.scalar.activation(upT[:, :, :].rearrange("p a l -> p (a l)"), sh_ps[:, 0:2 * DL], ACT.Copy
                                 ).then_inc(sh_read, 1)
            act.wait_ge(sh_full, 6)
            nc.scalar.activation(wqk[:, :, :].rearrange("p d (g l h) -> p (d g) h l", g=NKV, h=HG),
                                 sh_ps[:, :].rearrange("p (a h l) -> p a h l", h=HG, l=DL), ACT.Copy
                                 ).then_inc(sh_read, 1)
            act.wait_ge(sh_full, 7)
            nc.scalar.activation(wvo[:, :, :].rearrange("p g n -> p (g n)"), sh_ps[:, :], ACT.Copy
                                 ).then_inc(sh_read, 1)
            for n, name in enumerate(USES_START[7:], 7):
                read(name, n, -1, 1, 0)
            exps(0, 0, None)

            def batch(b, kind):
                for g in range(NKV):
                    w = b * 2 + g
                    no_before = kind == FIRST and g == 0
                    sums = [None if no_before else sum0_before(b, g, kind),
                            None if no_before else use_no(b, g, kind, "sum1")]
                    for e in range(NE):
                        names = list(USES_AT[kind][g][e])

                        def next_use():
                            if names:
                                name = names.pop(0)
                                read(name, use_no(b, g, kind, name), w, g, b + 1)

                        if e:
                            exps(w, e, sums[TILES[e][0]], next_use if ST_END[e] - ST_END[e - 1] > 2 else None)
                        if e == CT:
                            copy_u(w, 0)
                        next_use()
                        next_use()
                    if g == 0:
                        exps(b * 2 + 1, 0, use_no(b, 0, kind, "sum0"))
                    elif kind != LAST:
                        exps(b * 2 + 2, 0, use_no(b, 1, kind, "sum0"))
                    copy_u(w, 1)

            batch(0, FIRST)
            with act.Fori(1, B - 1) as b:
                batch(b, MID)
            batch(B - 1, LAST)
            read("sum1", USES_ALL, 0, 0, 0)

        @block.vector
        def _(dve):
            def maxima(w, n):
                t, h0, nh, own, width = MX[n]
                pitch = 2 * CH // nh if width * nh > CH else width
                dve.wait_ge(mx_full, w * NMX + (n + 1))
                nc.vector.tensor_reduce(mx_part[:, t // CT, own, h0:h0 + nh, t % CT],
                                        mx_ps[n % 2][:, 0:nh * pitch].rearrange("p (h k) -> p h k", h=nh)[:, :, 0:width],
                                        AX.X, ALU.max).then_inc(mx_free, 1)

            def split_max(w, c, uses_done):
                dve.wait_ge(mx_free, w * NMX + (NMX if c else MX_C0))
                dve.wait_ge(sh_full, uses_done)
                m = mx_part[:, 0, 1, :, :]
                if c:
                    nc.vector.tensor_tensor(mx_all[:, :, :], mx_part[:, 1, 0, :, :], mx_part[:, 1, 1, :, :], ALU.max
                                            ).then_inc(mx_step, 1)
                    dve.wait_ge(mx_step, w * 3 + 2)
                    m = mx_all[:, :, :]
                nc.vector.tensor_scalar(mx_split[:, 0, :, :], m, -1.0, None, ALU.mult).then_inc(mx_step, 1)
                dve.wait_ge(mx_step, w * 3 + (3 if c else 1))
                nc.vector.scalar_tensor_tensor(out=mx_split[:, 1, :, :], in0=m, scalar=-1.0,
                                               in1=mx_split[:, 0, :, :].bitcast(F), op0=ALU.mult, op1=ALU.subtract
                                               ).then_inc(max_ready, 1)

            def norm1_stats(bb, half, steps):
                for t in range(half * CT, (half + 1) * CT):
                    last = nc.vector.bn_stats(st1[:, t, :], x[:, bb, t, :])
                if half:
                    last.then_inc(ln_step, 1)
                    wait_apart(dve, (ln_step, steps + 1))
                    for t in range(TT):
                        last = nc.vector.bn_aggr(mv1[:, t, :], st1[:, t, :])
                    last.then_inc(ln_step, 1)
                    dve.wait_ge(ln_step, steps + 2)
                    nc.vector.tensor_scalar(var1[:, :], mv1[:, :, 1], EPS, None, ALU.add).then_inc(var_ready, 1)

            def norm1_apply(bb, powers):
                dve.wait_ge(rstd_ready, powers)
                for t in range(TT):
                    last = nc.vector.tensor_scalar(xn[:, t, :], x[:, bb, t, :], mv1[:, t, 0:1], rstd1[:, t:t + 1],
                                                   ALU.subtract, ALU.mult)
                last.then_inc(xn_ready, 1)

            def reciprocals(n):
                dve.wait_ge(sh_full, n + 1)
                nc.vector.reciprocal(r_q[:, :, :], sh_ps[:, :].rearrange("p (t h l) -> p t h l", t=CT, h=HG)[:, :, :, 0]
                                     ).then_inc(sh_read, 1)
                dve.wait_ge(sh_read, n + 1)
                nc.vector.tensor_copy(r_wide[:, :, :, :], r_q[:, :, :, None].to_broadcast([P, CT, HG, DL])
                                      ).then_inc(wide_ready, 1)

            def divide(w, g, c, n):
                dve.wait_ge(sh_full, n + 1)
                dve.wait_ge(u_read, u_count(w, c + 1))
                nc.vector.tensor_tensor(uT[g][:, c * CH:(c + 1) * CH], sh_ps[:, :], u_raw[:, :], ALU.mult
                                        ).then_inc(sh_read, 1)
                dve.wait_ge(sh_read, n + 1)
                dve.sem_inc(u_ready, 1)

            def residual(b, j, n):
                dve.wait_ge(sh_full, n + 1)
                two = x[:, b, 2 * j:2 * j + 2, :]
                nc.vector.tensor_tensor(two, sh_ps[:, :].rearrange("p (i d) -> p i d", i=2), two, ALU.add
                                        ).then_inc(sh_read, 1)
                wait_apart(dve, (sh_read, n + 1))
                for t in range(2 * j, 2 * j + 2):
                    last = nc.vector.bn_stats(st2[:, t % CT, :], x[:, b, t, :])
                if j % 2:
                    last.then_inc(ln_step, 1)

            def norm2_stats(steps):
                wait_apart(dve, (ln_step, steps + 1))
                for t in range(CT):
                    last = nc.vector.bn_aggr(mv2[:, t, :], st2[:, t, :])
                last.then_inc(ln_step, 1)
                dve.wait_ge(ln_step, steps + 2)
                nc.vector.tensor_scalar(var2[:, :], mv2[:, :, 1], 1.0 + EPS, EPS * EPS, ALU.mult, ALU.add
                                        ).then_inc(var_ready, 1)

            def norm2_apply(b, c, powers, steps):
                dve.wait_ge(out_done, y_count(b, c) * 16)
                for t in range(CT):
                    last = nc.vector.scalar_tensor_tensor(out=y[:, t, :], in0=x[:, b, c * CT + t, :], scalar=mv2[:, t, 0:1],
                                                          in1=lng[:, :], op0=ALU.subtract, op1=ALU.mult)
                last.then_inc(ln_step, 1)
                dve.wait_ge(ln_step, steps + 3)
                dve.wait_ge(rstd_ready, powers)
                dve.wait_ge(x1b_ready, b * NC + (c + 1))
                for t in range(CT):
                    last = nc.vector.scalar_tensor_tensor(out=y[:, t, :], in0=y[:, t, :], scalar=rstd2[:, t:t + 1],
                                                          in1=x1b[:, t, :], op0=ALU.mult, op1=ALU.add)
                last.then_inc(y_ready, 1)

            def low(name, n, nb):
                c = int(name[-1])
                kind = name.rstrip("0123456789")
                order = ["k0", "qa0", "k1", "qa1", "qb0", "qb1"]
                dve.wait_ge(sh_full, n + 1)
                dve.wait_ge(hi_ready, nb * len(order) + (order.index(name) + 1))
                s = slice(c * CH, (c + 1) * CH)
                if kind == "k":
                    nc.vector.tensor_tensor(k_lo[:, s], sh_ps[0:NKV * DL, :], k_hi[:, s].bitcast(F), ALU.subtract
                                            ).then_inc(sh_read, 1)
                else:
                    nc.vector.tensor_tensor(q_lo[:, s], sh_ps[:, :], q_hi[:, s].bitcast(F), ALU.subtract
                                            ).then_inc(sh_read, 1)

            dve.sem_inc(u_ready, U_AHEAD)
            dve.sem_inc(u_read, U_AHEAD)
            for g in range(NKV):
                nc.vector.memset(ks[g][KS:KM, :].bitcast(F), 1.0)
            nc.vector.memset(ones[:, :], 1.0)
            nc.vector.memset(minus_half[:, :], -0.5).then_inc(consts_ready, 1)
            dve.wait_ge(x0_in, 16)
            norm1_stats(0, 0, 0)
            norm1_stats(0, 1, 0)
            norm1_apply(0, 1)
            for n, name in enumerate(USES_START):
                if name[0] in "kq":
                    low(name, n, 0)
                if name == "m0":
                    for i in range(MX_C0):
                        maxima(0, i)
                    split_max(0, 0, n)
            for i in range(MX_C0, NMX):
                maxima(0, i)
            split_max(0, 1, USES_START.index("m0") + 1)
            dve.wait_ge(x_in, 16 * (B - 1))

            def use(name, b, g, kind):
                n = use_no(b, g, kind, name)
                w = b * 2 + g
                if name[0] in "kq":
                    low(name, n, b + 1)
                if name[:2] == "sT":
                    reciprocals(n)
                if name == "rT0":
                    divide(w, g, 0, n)
                if name == "rT1":
                    divide(w - 1, 1 - g, 1, n)
                if name[0] == "f":
                    residual(b - int(name[1]) // 2, int(name[1]), n)

            def batch(b, kind):
                steps, powers = (2, 1) if kind == FIRST else (b * 8 - 1, b * 3)
                for g in range(NKV):
                    w = b * 2 + g
                    wn = b * 2 + (g + 1)
                    no_m = kind == LAST and g == 1
                    for e in range(NE):
                        units = [] if no_m else list(range(MX_FROM[e], MX_FROM[e] + MX_AT[e]))
                        names = list(USES_AT[kind][g][e])
                        for part in range(4):
                            if part == 1 and names:
                                use(names.pop(0), b, g, kind)
                            if part != 1 and units:
                                maxima(wn, units.pop(0))
                            if part == 3 and names:
                                use(names.pop(0), b, g, kind)
                        if MX_FROM[e] < MX_C0 <= MX_FROM[e] + MX_AT[e] and not no_m:
                            split_max(wn, 0, use_no(b, g, kind, "m1") + 1)
                        if e == NE - 1 and not no_m:
                            split_max(wn, 1, use_no(b, g, kind, "m0") + 1)
                        if g == 0 and kind != LAST:
                            if e < 2:
                                norm1_stats(b + 1, e, steps)
                            if e == 2:
                                norm1_apply(b + 1, powers + 1)
                                steps, powers = steps + 2, powers + 1
                        if ("f3" if g == 0 else "f1") in USES_AT[kind][g][e]:
                            norm2_stats(steps)
                        if e == APPLY_AT[g] and (g or kind != FIRST):
                            norm2_apply(b - 1 if g == 0 else b, 1 - g, powers + 1, steps)
                            steps, powers = steps + 3, powers + 1
                return steps, powers

            batch(0, FIRST)
            with dve.Fori(1, B - 1) as b:
                batch(b, MID)
            steps, powers = batch(B - 1, LAST)
            reciprocals(USES_ALL + 1)
            divide(2 * B - 1, 1, 1, USES_ALL + 2)
            residual(B - 1, 2, USES_ALL + 3)
            residual(B - 1, 3, USES_ALL + 4)
            norm2_stats(steps)
            norm2_apply(B - 1, 1, powers + 1, steps)

        @block.gpsimd
        def _(pool):
            pool.sem_inc(pair_done, PAIRS_AHEAD)
            pool.sem_inc(y_ready, Y_AHEAD)
            pool.sem_inc(out_done, 16 * Y_AHEAD)
            nc.gpsimd.memset(ident[:, :], 0.0).then_inc(const_step, 1)
            nc.gpsimd.memset(maskb[:, :], 0.0).then_inc(const_step, 1)
            pool.wait_ge(const_step, 2)
            nc.gpsimd.affine_select(out=ident[:, :], in_=ident[:, :], compare_op=ALU.not_equal, fill=1.0, base=0,
                                    pattern=[[-1, P]], channel_multiplier=1).then_inc(const_step, 1)
            nc.gpsimd.affine_select(out=maskb[:, :], in_=maskb[:, :], compare_op=ALU.is_ge, fill=MASKED, base=0,
                                    pattern=[[-1, P]], channel_multiplier=1).then_inc(const_step, 1)
            pool.wait_ge(const_step, 4)
            nc.gpsimd.tensor_copy(identb[:, :], ident[:, :]).then_inc(consts_ready, 1)

            def rsqrt(out, in_, n, count):
                pool.wait_ge(var_ready, count)
                nc.gpsimd.tensor_tensor(out, in_, minus_half[:, 0:n], ALU.pow).then_inc(rstd_ready, 1)

            def diagonal(w, e):
                c, kt = TILES[e]
                off = first_query(c, kt)
                slot = e // 2 if e % 2 == 0 else 6 + (e // 2) % 2
                wait_apart(pool, (exp_done, w * NST + ST_END[e]))
                blk = pr[:, slot, :, off:off + P]
                nc.gpsimd.affine_select(out=blk, in_=blk, compare_op=ALU.is_ge, fill=0.0, base=0,
                                        pattern=[[0, HG], [1, P]], channel_multiplier=-1).then_inc(diag_done, 1)

            def pair(w, e):
                c, kt = TILES[e]
                off = first_query(c, kt)
                pool.wait_ge(pv_done, pv_count(w, e))
                if kt >= CT * c:
                    pool.wait_ge(diag_done, w * TT + (kt + 1))
                else:
                    pool.wait_ge(exp_done, w * NST + ST_END[e])
                even = pr[:, e // 2, :, off:CH]
                nc.gpsimd.tensor_tensor(even, even, pr[:, 6 + (e // 2) % 2, :, off:CH], ALU.add).then_inc(pair_done, 1)

            def take_v(g):
                nc.gpsimd.tensor_copy(v[g][:, :, :], v_both[:, :, g * DL:(g + 1) * DL]).then_inc(v_ready, 1)

            def add_bias(b, c, reads):
                pool.wait_ge(sh_read, reads)
                pool.wait_ge(y_ready, y_count(b, c))
                nc.gpsimd.tensor_tensor(x1b[:, :, :], x[:, b, c * CT:(c + 1) * CT, :], lnb[:, None, :].to_broadcast([P, CT, D]), ALU.add
                                        ).then_inc(x1b_ready, 1)

            pool.wait_ge(consts_ready, 2)
            pool.wait_ge(weights_in, 16 * 8)
            rsqrt(rstd1[:, :], var1[:, :], TT, 1)
            pool.wait_ge(sh_read, USES_START.index("v") + 1)
            take_v(0)
            take_v(1)
            diagonal(0, 0)

            def batch(b, kind):
                powers = 1 if kind == FIRST else b * 3
                for g in range(NKV):
                    w = b * 2 + g
                    for e in range(1, NE):
                        if g == 0 and e == 2 and kind != LAST:
                            rsqrt(rstd1[:, :], var1[:, :], TT, powers + 1)
                            powers = powers + 1
                        c, kt = TILES[e]
                        if kt >= CT * c:
                            diagonal(w, e)
                        if e % 2:
                            pair(w, e)
                        for name in USES_AT[kind][g][e]:
                            if name in ("f1", "f3"):
                                cc = int(name[1]) // 2
                                rsqrt(rstd2[:, :], var2[:, :], CT, powers + 1)
                                powers = powers + 1
                                add_bias(b - cc, cc, use_no(b, g, kind, name) + 1)
                    if not (kind == LAST and g == 1):
                        diagonal(b * 2 + (g + 1), 0)
                    if kind != LAST:
                        wait_apart(pool, (pv_done, pv_count(w, NE)),
                                   (sh_read, use_no(b, 0, kind, "v") + 1))
                        take_v(g)
                return powers

            batch(0, FIRST)
            with pool.Fori(1, B - 1) as b:
                batch(b, MID)
            powers = batch(B - 1, LAST)
            rsqrt(rstd2[:, :], var2[:, :], CT, powers + 1)
            add_bias(B - 1, 1, USES_ALL + len(USES_END))


def kernel(L0_attn_x, L0_attn_wq, L0_attn_wk_down, L0_attn_wv_down, L0_attn_wk_up, L0_attn_wv_up, L0_attn_wo,
           L0_ffn_ln_g, L0_ffn_ln_b, **unused):
    import numpy as np
    from concourse import bacc
    from concourse.bass_utils import run_bass_kernel_spmd

    nc = bacc.Bacc("TRN2", target_bir_lowering=False, num_devices=1)
    given = {"x": L0_attn_x, "wq": L0_attn_wq, "wk_down": L0_attn_wk_down, "wv_down": L0_attn_wv_down,
             "wk_up": L0_attn_wk_up, "wv_up": L0_attn_wv_up, "wo": L0_attn_wo,
             "ln_g": L0_ffn_ln_g, "ln_b": L0_ffn_ln_b}
    arrays, args = {}, []
    for name, a in given.items():
        a = np.ascontiguousarray(a)
        arrays[f"in_{name}"] = a
        args.append(nc.dram_tensor(f"in_{name}", a.shape, mybir.dt.from_np(a.dtype), kind="ExternalInput").ap())
    out = nc.dram_tensor("out_y", (B, T, D), mybir.dt.float32, kind="ExternalOutput").ap()
    program(nc, *args, out)
    result = run_bass_kernel_spmd(nc, [arrays], core_ids=[0])
    return result.results[0]["out_y"]
```

```python
from contextlib import ExitStack

import concourse.bass as bass
from concourse import mybir

B, T, D = 4, 1024, 256
NH, NKV, DH, DL = 8, 2, 128, 32
HG = NH // NKV
P = 128
TT = T // P
CH = 512
NC = T // CH
CT = CH // P
ND = D // P
KS = 3 * DL
KM = KS + 2
EPS = 1e-5
SCALE = DH ** -0.5
MASKED = -(2.0 ** 126)

TILES = [(c, kt) for c in range(NC) for kt in range(CT * (c + 1))]
NE = len(TILES)


def first_query(c, kt):
    return max(0, kt - CT * c) * P


def st_units():
    out = []
    for e, (c, kt) in enumerate(TILES):
        per = max(1, CH // (CH - first_query(c, kt)))
        per = 4 if per >= 4 else per
        out += [(e, h, per) for h in range(0, HG, per)]
    return out


ST = st_units()
NST = len(ST)
ST_END = [1 + max(n for n, u in enumerate(ST) if u[0] == e) for e in range(NE)]


def mx_units():
    out = []
    for t in range(TT):
        w = (t % CT + 1) * P
        per = HG if HG * w <= 2 * CH else 2
        out += [(t, h, per, 1, w) for h in range(0, HG, per)]
        if t >= CT:
            out += [(t, h, 2, 0, CH) for h in range(0, HG, 2)]
    return out


MX = mx_units()
NMX = len(MX)
MX_C0 = sum(u[0] < CT for u in MX)
MX_AT = [1, 1, 2, 1, 2, 2, 2, 2, 2, 2, 1, 2]
MX_AT_FIRST = [5, 5, 4, 3, 2, 3, 3, 3, 2, 2, 1, 1]


def mx_beside(kind, g, e):
    if kind == LAST and g == 1:
        return []
    if kind == FIRST and g == 0:
        todo = [(0, n) for n in range(MX_C0, NMX)] + [(1, n) for n in range(NMX)]
        at = MX_AT_FIRST
    else:
        todo, at = [(1, n) for n in range(NMX)], MX_AT
    return todo[sum(at[:e]):sum(at[:e + 1])]


def mx_share(left, part):
    return (len(left) if part == 3 else 1) if left and part != 1 else 0


FIRST, MID, LAST = 0, 1, 2
assert sum(MX_AT_FIRST) == 2 * NMX - MX_C0
assert sum(MX_AT) == NMX and NMX % 2 == 0 and NST % 2 == 0 and NE == 12

USES_START = ["wqT0", "wqT1", "wqT2", "wqT3", "upT", "wq", "xT0", "xT1", "k0", "qa0", "xT2", "xT3",
              "k1", "qa1", "wo", "v", "m0", "qb0", "qb1"]
SETUP = USES_START.index("xT0")
WINDOW0 = [["", ""], ["m1", "sum1"], ["sT1", "rT1"], ["", "xT0"], ["f2", "xT1"], ["f3", "m0"],
           ["sum0", "xT2"], ["sT0", "k0"], ["rT0", "xT3"], ["qa0", ""], ["k1", ""], ["qa1", ""]]
WINDOW1 = [["", ""], ["m1", "sum1"], ["sT1", ""], ["rT1", ""], ["", "v"], ["sum0", "sT0"],
           ["m0", "rT0"], ["qb0", "f0"], ["", "f1"], ["", "qb1"], ["", ""], ["", ""]]
WINDOW0_FIRST = [["", ""], ["", "xT0"], ["", "xT1"], ["m1", "xT2"], ["", "xT3"], ["sum0", ""],
                 ["sT0", "m0"], ["rT0", "k0"], ["", "qa0"], ["", "k1"], ["", "qa1"], ["", ""]]


def without(window, *names):
    return [["" if u in names else u for u in uses] for uses in window]


USES_AT = {
    FIRST: [WINDOW0_FIRST, WINDOW1],
    MID: [WINDOW0, WINDOW1],
    LAST: [without(WINDOW0, "xT0", "xT1", "xT2", "xT3", "k0", "k1", "qa0", "qa1"),
           without(WINDOW1, "qb0", "qb1", "v", "m0")],
}
USES_END = ["sum1", "sT1", "rT1", "f2", "f3"]
NORM1_AT = [(e, part) for e in range(4) for part in (0, 2)]
STATS_AFTER = ["xT0", "qa0", "qb1"]
NORMS1 = NC + B - 1
POOL_AT = {1: [("clear", 1), ("clear", 2), ("add", 1, 0, 2)],
           3: [("clear", 3), ("add", 1, 2, HG), ("add", 3, 0, HG)],
           5: [("add", 5, 0, HG)],
           7: [("clear", 8), ("add", 7, 0, 2)],
           9: [("clear", 9), ("add", 7, 2, HG)],
           11: [("clear", 10), ("add", 9, 0, 2), ("clear", 11), ("add", 9, 2, HG), ("clear", NE), ("add", 11, 0, HG)]}
APPLY0, APPLY0_END = 10, 1
APPLY1 = 7


def program(nc, x_d, wq_d, wkd_d, wvd_d, wku_d, wvu_d, wo_d, lng_d, lnb_d, out_d):
    F, R, BF = mybir.dt.float32, mybir.dt.float32r, mybir.dt.bfloat16
    ACT, ALU, AX = mybir.ActivationFunctionType, mybir.AluOpType, mybir.AxisListType

    with ExitStack() as ctx:
        def sb(name, shape, dtype=F):
            return ctx.enter_context(nc.sbuf_tensor(name, shape, dtype))

        def ps(name, shape, dtype=F):
            return ctx.enter_context(nc.psum_tensor(name, shape, dtype))

        def sem(name):
            return ctx.enter_context(nc.semaphore(name))

        ident = sb("ident", [P, P])
        identb = sb("identb", [P, P], BF)
        maskb = sb("maskb", [P, P], BF)
        ones = sb("ones", [P, DL])
        minus_half = sb("minus_half", [P, B * TT])
        lng = sb("lng", [P, D])
        lnb = sb("lnb", [P, D])
        wqk = sb("wqk", [P, ND, NH * DL])
        wkd = sb("wkd", [P, ND, NKV * DL])
        wvd = sb("wvd", [P, ND, NKV * DL])
        wvo = sb("wvo", [P, NKV, D])
        upT = sb("upT", [P, 2, DL])
        up = sb("up", [DL, 2, DH])
        x = sb("x", [P, B, TT, D])
        xn = sb("xn", [P, TT, D])
        xnT = sb("xnT", [P, ND, T])
        q_hi = sb("q_hi", [P, T], R)
        q_lo = sb("q_lo", [P, T], R)
        k_hi = sb("k_hi", [NKV * DL, T], R)
        k_lo = sb("k_lo", [NKV * DL, T], R)
        v_both = sb("v_both", [P, TT, NKV * DL])
        qs = [sb(f"qs{g}", [KM, NC, HG, CH], R) for g in range(NKV)]
        ks = [sb(f"ks{g}", [KM, T], R) for g in range(NKV)]
        v = [sb(f"v{g}", [P, TT, DL]) for g in range(NKV)]
        pr = sb("pr", [P, 8, HG, CH])
        u_raw = sb("u_raw", [P, CH])
        s_raw = sb("s_raw", [P, CH])
        r_q = sb("r_q", [P, CT, HG])
        r_wide = sb("r_wide", [P, CT, HG, DL])
        uT = [sb(f"uT{g}", [P, T]) for g in range(NKV)]
        mx_part = sb("mx_part", [P, NC, 2, HG, CT])
        mx_all = sb("mx_all", [P, HG, CT])
        mx_split = sb("mx_split", [P, 2, HG, CT], R)
        mx_row = sb("mx_row", [2 * HG * CT, P], R)
        st1 = sb("st1", [P, B, TT, 6])
        mv1 = sb("mv1", [P, B, TT, 2])
        var1 = sb("var1", [P, B, TT])
        rstd1 = sb("rstd1", [P, B, TT])
        st2 = sb("st2", [P, CT, 6])
        mv2 = sb("mv2", [P, CT, 2])
        var2 = sb("var2", [P, CT])
        rstd2 = sb("rstd2", [P, CT])
        x1b = sb("x1b", [P, CT, D])
        y = sb("y", [P, CT, D])
        wq_in_sb = pr[:, 0, :, :].rearrange("p a b -> p (a b)").rearrange("p (c n) -> p c n", c=ND)
        wo_in = pr[:, 1, :, :].rearrange("p a b -> p (a b)").rearrange("p (h n) -> p h n", h=NH)
        wqT = pr[:, 2, :, :].rearrange("p a b -> p (a b)").rearrange("p (h n) -> p h n", h=NH)

        mx_ps = [ps(f"mx_ps{i}", [P, 2 * CH]) for i in range(2)]
        st_ps = [ps(f"st_ps{i}", [P, CH]) for i in range(2)]
        u_ps = ps("u_ps", [P, CH])
        sh_ps = ps("sh_ps", [P, CH])
        start_ps = [sh_ps, st_ps[0], st_ps[1], u_ps]

        weights_in = sem("weights_in")
        wq_in = sem("wq_in")
        wo_loaded = sem("wo_loaded")
        ln_in = sem("ln_in")
        x0_in = [sem(f"x0_in{c}") for c in range(NC)]
        x_in = [sem(f"x_in{b}") for b in range(1, B)]
        const_step = sem("const_step")
        consts_ready = sem("consts_ready")
        sh_full = sem("sh_full")
        sh_read = sem("sh_read")
        start_read = [sem(f"start_read{i}") for i in range(4)]
        hi_ready = sem("hi_ready")
        mx_full = sem("mx_full")
        mx_free = sem("mx_free")
        mx_step = sem("mx_step")
        max_ready = sem("max_ready")
        rows_in = sem("rows_in")
        st_full = sem("st_full")
        exp_done = sem("exp_done")
        diag_done = sem("diag_done")
        pair_done = sem("pair_done")
        pv_done = sem("pv_done")
        u_read = sem("u_read")
        wide_ready = sem("wide_ready")
        u_ready = sem("u_ready")
        v_ready = sem("v_ready")
        qstack_in = [[sem(f"qstack_in{g}{c}") for c in range(NC)] for g in range(NKV)]
        kstack_in = [[sem(f"kstack_in{g}{c}") for c in range(NC)] for g in range(NKV)]
        ln_step = sem("ln_step")
        var_ready = sem("var_ready")
        rstd_ready = sem("rstd_ready")
        xn_ready = sem("xn_ready")
        x1_ready = sem("x1_ready")
        x1b_ready = sem("x1b_ready")
        y_ready = sem("y_ready")
        out_done = sem("out_done")
        carrier = sem("carrier")

        def flat(table):
            return [name for e in range(NE) for name in table[e] if name]

        def wait_apart(eng, *waits):
            for s, v in waits:
                eng.wait_ge(s, v)
                eng.sem_inc(carrier, 1)

        PV_AHEAD, PAIRS_AHEAD, U_AHEAD, Y_AHEAD = 3, 2, 1, 1

        def pv_count(w, tiles):
            return w * NE + (PV_AHEAD + tiles)

        def pair_count(w, pairs):
            return w * (NE // 2) + (PAIRS_AHEAD + pairs)

        def u_count(w, chunks):
            return w * NC + (U_AHEAD + chunks)

        def y_count(b, chunks):
            return b * NC + (Y_AHEAD + chunks)

        def uses_of(kind):
            return sum(len(flat(USES_AT[kind][g])) for g in range(NKV))

        def uses_before(b):
            if isinstance(b, int) and b == 0:
                return 0
            return (b - 1) * uses_of(MID) + uses_of(FIRST)

        def start_bank(name):
            return start_ps[USES_START.index(name) % len(start_ps)]

        def start_sem(name):
            return start_read[USES_START.index(name) % len(start_ps)]

        def start_full(name):
            return USES_START.index(name) + 1

        def wait_start(eng, name):
            eng.wait_ge(start_sem(name), USES_START.index(name) // len(start_ps) + 1)

        def sh_fills(n):
            return n + (len(USES_START) + 1)

        def use_no(b, g, kind, name):
            before = len(flat(USES_AT[kind][0])) if g else 0
            return uses_before(b) + (before + flat(USES_AT[kind][g]).index(name))

        USES_ALL = uses_before(B - 1) + uses_of(LAST)

        def sum0_before(b, g, kind):
            if g:
                return use_no(b, 0, kind, "sum0")
            names = flat(USES_AT[MID][1])
            return uses_before(b) - (len(names) - names.index("sum0"))

        block = ctx.enter_context(nc.Block())

        @block.sync
        def _(sp):
            for c in range(NC):
                sp.dma_start(x[:, 0, c * CT:(c + 1) * CT, :],
                             x_d.rearrange("b (c t p) d -> b c p t d", c=NC, p=P)[0, c]).then_inc(x0_in[c], 16)
            sp.dma_start(up[:, 0, :], wku_d).then_inc(weights_in, 16)
            sp.dma_start(up[:, 1, :], wvu_d).then_inc(weights_in, 16)
            sp.dma_start(wkd[:, :, :], wkd_d.rearrange("(c p) n -> p c n", p=P)).then_inc(weights_in, 16)
            sp.dma_start(wvd[:, :, :], wvd_d.rearrange("(c p) n -> p c n", p=P)).then_inc(weights_in, 16)
            sp.dma_start(wo_in, wo_d.rearrange("(h p) n -> p h n", p=P)).then_inc(wo_loaded, 16)
            for b in range(1, B):
                sp.dma_start(x[:, b, :, :], x_d[b].rearrange("(t p) d -> p t d", p=P)).then_inc(x_in[b - 1], 16)
            sp.dma_start(lng[:, :], lng_d[None, :].to_broadcast([P, D])).then_inc(ln_in, 16)
            sp.dma_start(lnb[:, :], lnb_d[None, :].to_broadcast([P, D])).then_inc(ln_in, 16)

            def stack_q(g, c):
                s = slice(c * CH, (c + 1) * CH)
                for piece, src in enumerate((q_hi, q_hi, q_lo)):
                    sp.dma_start(qs[g][piece * DL:(piece + 1) * DL, c, :, :].bitcast(F), src[:, s].bitcast(F)
                                 ).then_inc(qstack_in[g][c], 16)

            def stack_k(g, c):
                s = slice(c * CH, (c + 1) * CH)
                for piece, src in enumerate((k_hi, k_lo, k_hi)):
                    sp.dma_start(ks[g][piece * DL:(piece + 1) * DL, s].bitcast(F),
                                 src[g * DL:(g + 1) * DL, s].bitcast(F)).then_inc(kstack_in[g][c], 16)

            wait_start(sp, "k0")
            stack_k(0, 0)
            wait_start(sp, "qa0")
            stack_q(0, 0)
            wait_start(sp, "k1")
            stack_k(0, 1)
            wait_start(sp, "qa1")
            stack_q(0, 1)
            stack_k(1, 0)
            stack_k(1, 1)
            wait_start(sp, "qb0")
            stack_q(1, 0)
            wait_start(sp, "qb1")
            stack_q(1, 1)

            def batch(b, kind):
                w = b * 2
                if kind != FIRST:
                    put(b - 1, 0)
                    put(b - 1, 1)
                wait_apart(sp, (st_full, w * NST + ST_END[7]),
                           (sh_read, use_no(b, 0, kind, "k0") + 1))
                stack_k(0, 0)
                wait_apart(sp, (sh_read, use_no(b, 0, kind, "qa0") + 1))
                stack_q(0, 0)
                wait_apart(sp, (st_full, w * NST + NST),
                           (sh_read, use_no(b, 0, kind, "k1") + 1))
                stack_k(0, 1)
                wait_apart(sp, (sh_read, use_no(b, 0, kind, "qa1") + 1))
                stack_q(0, 1)
                wait_apart(sp, (st_full, w * NST + (NST + ST_END[3])),
                           (sh_read, use_no(b, 1, kind, "qb0") + 1))
                stack_q(1, 0)
                wait_apart(sp, (st_full, w * NST + (NST + ST_END[7])))
                stack_k(1, 0)
                wait_apart(sp, (st_full, w * NST + 2 * NST))
                stack_k(1, 1)
                wait_apart(sp, (sh_read, use_no(b, 1, kind, "qb1") + 1))
                stack_q(1, 1)

            def put(b, c):
                wait_apart(sp, (y_ready, y_count(b, c + 1)))
                sp.dma_start(out_d.rearrange("b (c t p) d -> b c p t d", c=NC, p=P)[b, c], y[:, :, :]
                             ).then_inc(out_done, 16)

            batch(0, FIRST)
            with sp.Fori(1, B - 1) as b:
                batch(b, MID)
            put(B - 2, 0)
            put(B - 2, 1)
            put(B - 1, 0)
            put(B - 1, 1)
            sp.wait_ge(out_done, 16 * y_count(B, 0))

        @block.tensor
        def _(pe):
            def shared(n):
                if isinstance(n, int) and n == 0:
                    wait_start(pe, USES_START[(len(USES_START) - 1) // 4 * 4])
                else:
                    pe.wait_ge(sh_read, n)

            def starting(name):
                i = USES_START.index(name)
                if i >= len(start_ps):
                    wait_start(pe, USES_START[i - len(start_ps)])

            def st(w, g, n):
                e, h0, nh = ST[n]
                c, kt = TILES[e]
                off = first_query(c, kt)
                width = CH - off
                if n == 0 or ST[n - 1][0] != e:
                    if kt == 0:
                        pe.wait_ge(rows_in, w * 64 + 32 * (c + 1))
                if not (isinstance(w, int) and w == 0 and n < 2):
                    pe.wait_ge(exp_done, w * NST + (n - 1))
                nc.tensor.matmul(st_ps[n % 2][:, 0:nh * width], ks[g][0:KM, kt * P:(kt + 1) * P],
                                 qs[g][0:KM, c, h0:h0 + nh, off:CH], start=True, stop=True).then_inc(st_full, 1)

            def mx(w, bb, g, n):
                t, h0, nh, own, width = MX[n]
                if n == 0:
                    pe.wait_ge(qstack_in[g][0], (bb + 1) * 16 * 3)
                    pe.wait_ge(kstack_in[g][0], (bb + 1) * 16 * 3)
                if n == MX_C0:
                    pe.wait_ge(qstack_in[g][1], (bb + 1) * 16 * 3)
                    pe.wait_ge(kstack_in[g][1], (bb + 1) * 16 * 3)
                if not (isinstance(w, int) and w == 0 and n < 2):
                    pe.wait_ge(mx_free, w * NMX + (n - 1))
                pitch = 2 * CH // nh if width * nh > CH else width
                k0 = (t // CT) * CH if own else 0
                bank = mx_ps[n % 2]
                for i in range(nh):
                    last = nc.tensor.matmul(bank[:, i * pitch:i * pitch + width],
                                            qs[g][0:KS, t // CT, h0 + i, t % CT * P:(t % CT + 1) * P],
                                            ks[g][0:KS, k0:k0 + width], start=True, stop=not own)
                    if own:
                        last = nc.tensor.matmul(bank[:, i * pitch + width - P:i * pitch + width],
                                                identb[:, :], maskb[:, :], start=False, stop=True)
                last.then_inc(mx_full, 1)

            def pv(w, g, e):
                c, kt = TILES[e]
                off = first_query(c, kt)
                slot = e // 2 if e % 2 == 0 else 6 + (e // 2) % 2
                if e == 0:
                    pe.wait_ge(v_ready, w + 1)
                if kt == 0 and not (isinstance(w, int) and w == 0 and c == 0):
                    pe.wait_ge(u_read, u_count(w, c))
                if kt >= CT * c:
                    pe.wait_ge(diag_done, w * TT + (kt + 1))
                else:
                    pe.wait_ge(exp_done, w * NST + ST_END[e])
                for h in range(HG):
                    last = nc.tensor.matmul(u_ps[h * DL:(h + 1) * DL, off:CH], v[g][:, kt, :],
                                            pr[:, slot, h, off:CH], start=kt == 0, stop=kt == CT * (c + 1) - 1)
                last.then_inc(pv_done, 1)

            def sums(w, c):
                pairs = [e for e in range(0, NE, 2) if TILES[e][0] == c]
                for e in pairs:
                    off = first_query(*TILES[e])
                    pe.wait_ge(pair_done, pair_count(w, e // 2 + 1))
                    for h in range(HG):
                        last = nc.tensor.matmul(sh_ps[h * DL:(h + 1) * DL, off:CH], ones[:, :],
                                                pr[:, e // 2, h, off:CH], start=e == pairs[0], stop=e == pairs[-1])
                return last

            def fill(name, n, w, wn, nb):
                bank = sh_ps
                if n is None:
                    starting(name)
                    bank = start_bank(name)
                else:
                    shared(n)
                c = int(name[-1]) if name[-1].isdigit() else 0
                kind = name.rstrip("0123456789")
                if kind == "xT":
                    pe.wait_ge(xn_ready, nb * TT + (2 * c + 2))
                    for i in range(2):
                        for d in range(ND):
                            j = 2 * i + d
                            last = nc.tensor.transpose(bank[:, j * P:(j + 1) * P],
                                                       xn[:, 2 * c + i, d * P:(d + 1) * P], ident[:, :])
                elif kind == "k":
                    if n is None:
                        pe.wait_ge(weights_in, 4 * 16)
                        wait_start(pe, f"xT{2 * c}")
                        wait_start(pe, f"xT{2 * c + 1}")
                    for d in range(ND):
                        last = nc.tensor.matmul(bank[0:NKV * DL, :], wkd[:, d, :],
                                                xnT[:, d, c * CH:(c + 1) * CH], start=d == 0, stop=d == ND - 1)
                elif kind in ("qa", "qb"):
                    if n is None:
                        wait_start(pe, "wq")
                    for d in range(ND):
                        gq = 0 if kind == "qa" else 1
                        last = nc.tensor.matmul(bank[:, :], wqk[:, d, gq * P:(gq + 1) * P],
                                                xnT[:, d, c * CH:(c + 1) * CH], start=d == 0, stop=d == ND - 1)
                elif kind == "v":
                    for t in range(TT):
                        for d in range(ND):
                            last = nc.tensor.matmul(bank[:, t * NKV * DL:(t + 1) * NKV * DL],
                                                    xnT[:, d, t * P:(t + 1) * P], wvd[:, d, :],
                                                    start=d == 0, stop=d == ND - 1)
                elif kind == "m":
                    pe.wait_ge(max_ready, wn * NC + 1 if c == 0 else w * NC + 2)
                    last = nc.tensor.transpose(bank[0:2 * HG * CT, 0:P],
                                               mx_split[:, :, :, :].rearrange("p a h t -> p (a h t)").bitcast(F),
                                               ident[:, :])
                elif kind == "sum":
                    last = sums(w - c, c)
                elif kind == "sT":
                    for t in range(CT):
                        last = nc.tensor.transpose(bank[:, t * P:(t + 1) * P], s_raw[:, t * P:(t + 1) * P],
                                                   ident[:, :])
                elif kind == "rT":
                    pe.wait_ge(wide_ready, w * NC + (1 - c))
                    for t in range(CT):
                        last = nc.tensor.transpose(bank[:, t * P:(t + 1) * P],
                                                   r_wide[:, t, :, :].rearrange("p h l -> p (h l)"), ident[:, :])
                else:
                    if c == 0:
                        pe.wait_ge(u_ready, u_count(w, 1))
                    if c == 2:
                        pe.wait_ge(u_ready, u_count(w - 1, 2))
                    for i in range(2):
                        t = 2 * c + i
                        for gg in range(NKV):
                            last = nc.tensor.matmul(bank[:, i * D:(i + 1) * D], uT[gg][:, t * P:(t + 1) * P],
                                                    wvo[:, gg, :], start=gg == 0, stop=gg == NKV - 1)
                last.then_inc(sh_full, 1)

            pe.sem_inc(pv_done, PV_AHEAD)
            pe.wait_ge(consts_ready, 2)
            pe.wait_ge(wq_in, 16)
            for n in range(4):
                starting(f"wqT{n}")
                for i in range(2):
                    for d in range(ND):
                        j = 2 * i + d
                        last = nc.tensor.transpose(start_bank(f"wqT{n}")[:, j * P:(j + 1) * P],
                                                   wq_in_sb[:, d, (2 * n + i) * DH:(2 * n + i + 1) * DH], ident[:, :])
                last.then_inc(sh_full, 1)
            pe.wait_ge(weights_in, 4 * 16)
            starting("upT")
            for i in range(2):
                last = nc.tensor.transpose(start_bank("upT")[:, i * DL:(i + 1) * DL], up[:, i, :], ident[0:DL, 0:DL])
            last.then_inc(sh_full, 1)
            starting("wq")
            wait_start(pe, "wqT3")
            wait_start(pe, "wqT2")
            wait_start(pe, "upT")
            for d in range(ND):
                for h in range(NH):
                    last = nc.tensor.matmul(start_bank("wq")[:, d * D + h * DL:d * D + (h + 1) * DL],
                                            wqT[:, h, d * P:(d + 1) * P], upT[:, 0, :], start=True, stop=True)
            last.then_inc(sh_full, 1)

            for name in USES_START[SETUP:]:
                if name == "wo":
                    for i in range(MX_C0):
                        mx(0, 0, 0, i)
                    starting("wo")
                    pe.wait_ge(wo_loaded, 16)
                    for h in range(NH):
                        gg, j = h // HG, h % HG
                        last = nc.tensor.matmul(start_bank("wo")[j * DL:(j + 1) * DL, gg * D:(gg + 1) * D],
                                                upT[:, 1, :], wo_in[:, h, :], start=True, stop=True)
                    last.then_inc(sh_full, 1)
                    continue
                fill(name, None, 0, 0, 0)
            wait_start(pe, USES_START[-2])
            wait_start(pe, USES_START[-1])
            for n in range(ST_END[0]):
                st(0, 0, n)

            def batch(b, kind):
                for g in range(NKV):
                    w = b * 2 + g
                    wn = b * 2 + (g + 1)
                    no_m = kind == LAST and g == 1
                    for e in range(NE):
                        units = list(range(ST_END[e - 1], ST_END[e])) if e else []
                        after = []
                        if e == NE - 1 and not no_m:
                            after = list(range(ST_END[0]))
                        beside = mx_beside(kind, g, e)
                        names = USES_AT[kind][g][e]
                        for part in range(4):
                            if units:
                                st(w, g, units.pop(0))
                            elif after and part >= 2:
                                st(wn, 1 - g, after.pop(0))
                            if part == 1 and names[0]:
                                fill(names[0], use_no(b, g, kind, names[0]), w, wn, b + 1)
                            if part == 1 and e:
                                pv(w, g, e - 1)
                            for _ in range(mx_share(beside, part)):
                                ahead, n = beside.pop(0)
                                if ahead:
                                    mx(wn, b + g, 1 - g, n)
                                else:
                                    mx(w, b, g, n)
                            if part == 3 and names[1]:
                                fill(names[1], use_no(b, g, kind, names[1]), w, wn, b + 1)
                    if after:
                        st(wn, 1 - g, after.pop(0))
                    pv(w, g, NE - 1)
                    for n in after:
                        st(wn, 1 - g, n)

            batch(0, FIRST)
            with pe.Fori(1, B - 1) as b:
                batch(b, MID)
            batch(B - 1, LAST)
            for i, name in enumerate(USES_END):
                fill(name, USES_ALL + i, 2 * B, 0, 0)

        @block.scalar
        def _(act):
            def exps(w, e, sum_before, between=None):
                c, kt = TILES[e]
                off = first_query(c, kt)
                width = CH - off
                slot = e // 2 if e % 2 == 0 else 6 + (e // 2) % 2
                first = isinstance(w, int) and w == 0
                if e % 2 == 0:
                    if not first:
                        act.wait_ge(sh_full, sh_fills(sum_before))
                elif not (first and e < 4):
                    act.wait_ge(pv_done, pv_count(w, e - 3))
                    act.wait_ge(pair_done, pair_count(w, e // 2 - 1))
                n0 = ST_END[e - 1] if e else 0
                for n in range(n0, ST_END[e]):
                    _, h0, nh = ST[n]
                    if n == n0 + 2 and between:
                        between()
                    act.wait_ge(st_full, w * NST + (n + 1))
                    nc.scalar.activation(pr[:, slot, h0:h0 + nh, off:CH],
                                         st_ps[n % 2][:, 0:nh * width].rearrange("p (h q) -> p h q", h=nh),
                                         ACT.Exp, scale=SCALE).then_inc(exp_done, 1)

            def copy_u(w, c):
                act.wait_ge(pv_done, pv_count(w, CT if c == 0 else NE))
                if not (isinstance(w, int) and w == 0 and c == 0):
                    act.wait_ge(u_ready, u_count(w, c))
                nc.scalar.activation(u_raw[:, :], u_ps[:, :], ACT.Copy).then_inc(u_read, 1)

            def take_v():
                for g in range(NKV):
                    nc.scalar.activation(v[g][:, :, :], v_both[:, :, g * DL:(g + 1) * DL], ACT.Copy).then_inc(v_ready, 1)

            def read(name, n, w, g, nb):
                bank = sh_ps if n is not None else start_bank(name)
                done = sh_read if n is not None else start_sem(name)
                c = int(name[-1]) if name[-1].isdigit() else 0
                kind = name.rstrip("0123456789")
                if kind in ("sT", "rT", "f"):
                    return
                act.wait_ge(sh_full, start_full(name) if n is None else sh_fills(n))
                if kind == "xT":
                    dst = xnT[:, :, 2 * c * P:2 * (c + 1) * P].rearrange("p d (i q) -> p i d q", i=2)
                    nc.scalar.activation(dst, bank[:, :].rearrange("p (i d q) -> p i d q", i=2, d=ND), ACT.Copy
                                         ).then_inc(done, 1)
                elif kind == "k":
                    for gg in range(NKV):
                        if not (isinstance(nb, int) and nb == 0):
                            act.wait_ge(kstack_in[gg][c], nb * 16 * 3)
                    nc.scalar.activation(k_hi[:, c * CH:(c + 1) * CH], bank[0:NKV * DL, :], ACT.Copy
                                         ).then_inc(hi_ready, 1)
                elif kind in ("qa", "qb"):
                    if kind == "qb":
                        act.wait_ge(qstack_in[0][c], (nb + 1) * 16 * 3)
                    elif not (isinstance(nb, int) and nb == 0):
                        act.wait_ge(qstack_in[1][c], nb * 16 * 3)
                    nc.scalar.activation(q_hi[:, c * CH:(c + 1) * CH], bank[:, :], ACT.Copy
                                         ).then_inc(hi_ready, 1)
                elif kind == "sum":
                    nc.scalar.activation(s_raw[:, :], bank[:, :], ACT.Copy).then_inc(done, 1)
                elif kind == "v":
                    if not (isinstance(nb, int) and nb == 0):
                        act.wait_ge(v_ready, nb * 2)
                    nc.scalar.activation(v_both[:, :, :].rearrange("p t n -> p (t n)"), bank[:, :], ACT.Copy
                                         ).then_inc(done, 1)
                else:
                    wm, gm = (w + 1, 1 - g) if c == 0 else (w, g)
                    if not (isinstance(wm, int) and wm == 0 and c == 0):
                        act.wait_ge(rows_in, wm * 64 + 32 * c)
                    nc.scalar.activation(mx_row[:, :], bank[0:2 * HG * CT, 0:P], ACT.Copy).then_inc(done, 1)
                    if n is None:
                        wait_start(act, name)
                    else:
                        act.wait_ge(sh_read, n + 1)
                    for part in range(2):
                        act.dma_start(qs[gm][KS + part:KS + part + 1, c, :, :].rearrange("p h q -> p (h q)")
                                      .rearrange("p (r q) -> p r q", q=P).bitcast(F),
                                      mx_row[part * HG * CT:(part + 1) * HG * CT, :].bitcast(F)
                                      ).then_inc(rows_in, 16)

            act.dma_start(wq_in_sb, wq_d.rearrange("(c p) n -> p c n", p=P)).then_inc(wq_in, 16)

            def setup(name, dst, src):
                act.wait_ge(sh_full, start_full(name))
                nc.scalar.activation(dst, src, ACT.Copy).then_inc(start_sem(name), 1)

            for n in range(4):
                setup(f"wqT{n}", wqT[:, 2 * n:2 * n + 2, :].rearrange("p h n -> p (h n)"), start_bank(f"wqT{n}")[:, :])
            setup("upT", upT[:, :, :].rearrange("p a l -> p (a l)"), start_bank("upT")[:, 0:2 * DL])
            setup("wq", wqk[:, :, :].rearrange("p d (g l h) -> p (d g) h l", g=NKV, h=HG),
                  start_bank("wq")[:, :].rearrange("p (a h l) -> p a h l", h=HG, l=DL))
            for name in USES_START[SETUP:]:
                if name == "wo":
                    setup("wo", wvo[:, :, :].rearrange("p g n -> p (g n)"), start_bank("wo")[:, :])
                else:
                    read(name, None, -1, 1, 0)
                if name == "m0":
                    wait_start(act, "v")
                    take_v()
            exps(0, 0, None)

            def batch(b, kind):
                for g in range(NKV):
                    w = b * 2 + g
                    no_before = kind == FIRST and g == 0
                    sums = [None if no_before else sum0_before(b, g, kind),
                            None if no_before else use_no(b, g, kind, "sum1")]
                    for e in range(NE):
                        names = USES_AT[kind][g][e]

                        def read_use(name):
                            if name:
                                read(name, use_no(b, g, kind, name), w, g, b + 1)

                        if e:
                            many = ST_END[e] - ST_END[e - 1] > 2
                            exps(w, e, sums[TILES[e][0]], (lambda: read_use(names[0])) if many else None)
                            if not many:
                                read_use(names[0])
                        if e == CT:
                            copy_u(w, 0)
                        read_use(names[1])
                    if g == 0:
                        exps(b * 2 + 1, 0, use_no(b, 0, kind, "sum0"))
                    elif kind != LAST:
                        exps(b * 2 + 2, 0, use_no(b, 1, kind, "sum0"))
                    copy_u(w, 1)
                    if g and kind != LAST:
                        act.wait_ge(sh_read, use_no(b, 1, kind, "v") + 1)
                        take_v()

            batch(0, FIRST)
            with act.Fori(1, B - 1) as b:
                batch(b, MID)
            batch(B - 1, LAST)
            read("sum1", USES_ALL, 0, 0, 0)

        @block.vector
        def _(dve):
            def maxima(w, n):
                t, h0, nh, own, width = MX[n]
                pitch = 2 * CH // nh if width * nh > CH else width
                dve.wait_ge(mx_full, w * NMX + (n + 1))
                nc.vector.tensor_reduce(mx_part[:, t // CT, own, h0:h0 + nh, t % CT],
                                        mx_ps[n % 2][:, 0:nh * pitch].rearrange("p (h k) -> p h k", h=nh)[:, :, 0:width],
                                        AX.X, ALU.max).then_inc(mx_free, 1)

            def split_max(w, c, uses_done):
                dve.wait_ge(mx_free, w * NMX + (NMX if c else MX_C0))
                if not (isinstance(uses_done, int) and uses_done == 0):
                    dve.wait_ge(sh_full, uses_done)
                m = mx_part[:, 0, 1, :, :]
                if c:
                    nc.vector.tensor_tensor(mx_all[:, :, :], mx_part[:, 1, 0, :, :], mx_part[:, 1, 1, :, :], ALU.max
                                            ).then_inc(mx_step, 1)
                    dve.wait_ge(mx_step, w * 3 + 2)
                    m = mx_all[:, :, :]
                nc.vector.tensor_scalar(mx_split[:, 0, :, :], m, -1.0, None, ALU.mult).then_inc(mx_step, 1)
                dve.wait_ge(mx_step, w * 3 + (3 if c else 1))
                nc.vector.scalar_tensor_tensor(out=mx_split[:, 1, :, :], in0=m, scalar=-1.0,
                                               in1=mx_split[:, 0, :, :].bitcast(F), op0=ALU.mult, op1=ALU.subtract
                                               ).then_inc(max_ready, 1)

            def norm1_stats(b, tiles, count):
                for t in tiles:
                    last = nc.vector.bn_stats(st1[:, b, t, :], x[:, b, t, :])
                last.then_inc(ln_step, 1)
                dve.wait_ge(ln_step, 2 * count - 1)
                for t in tiles:
                    last = nc.vector.bn_aggr(mv1[:, b, t, :], st1[:, b, t, :])
                last.then_inc(ln_step, 1)
                dve.wait_ge(ln_step, 2 * count)
                nc.vector.tensor_scalar(var1[:, b, tiles[0]:tiles[-1] + 1], mv1[:, b, tiles[0]:tiles[-1] + 1, 1], EPS, None,
                                        ALU.add).then_inc(var_ready, 1)

            def norm1_apply(bb, t):
                nc.vector.tensor_scalar(xn[:, t, :], x[:, bb, t, :], mv1[:, bb, t, 0:1],
                                        rstd1[:, bb, t:t + 1], ALU.subtract, ALU.mult).then_inc(xn_ready, 1)

            def reciprocals(n):
                dve.wait_ge(sh_full, sh_fills(n))
                nc.vector.reciprocal(r_q[:, :, :], sh_ps[:, :].rearrange("p (t h l) -> p t h l", t=CT, h=HG)[:, :, :, 0]
                                     ).then_inc(sh_read, 1)
                dve.wait_ge(sh_read, n + 1)
                nc.vector.tensor_copy(r_wide[:, :, :, :], r_q[:, :, :, None].to_broadcast([P, CT, HG, DL])
                                      ).then_inc(wide_ready, 1)

            def divide(w, g, c, n):
                dve.wait_ge(sh_full, sh_fills(n))
                dve.wait_ge(u_read, u_count(w, c + 1))
                nc.vector.tensor_tensor(uT[g][:, c * CH:(c + 1) * CH], sh_ps[:, :], u_raw[:, :], ALU.mult
                                        ).then_inc(sh_read, 1)
                dve.wait_ge(sh_read, n + 1)
                dve.sem_inc(u_ready, 1)

            def residual(b, j, n):
                dve.wait_ge(sh_full, sh_fills(n))
                two = x[:, b, 2 * j:2 * j + 2, :]
                nc.vector.tensor_tensor(two, sh_ps[:, :].rearrange("p (i d) -> p i d", i=2), two, ALU.add
                                        ).then_inc(sh_read, 1)
                wait_apart(dve, (sh_read, n + 1))
                for t in range(2 * j, 2 * j + 2):
                    last = nc.vector.bn_stats(st2[:, t % CT, :], x[:, b, t, :])
                if j % 2:
                    last.then_inc(ln_step, 1)

            def norm2_stats(steps):
                wait_apart(dve, (ln_step, steps + 1))
                for t in range(CT):
                    last = nc.vector.bn_aggr(mv2[:, t, :], st2[:, t, :])
                last.then_inc(ln_step, 1)
                dve.wait_ge(ln_step, steps + 2)
                nc.vector.tensor_scalar(var2[:, :], mv2[:, :, 1], 1.0 + EPS, EPS * EPS, ALU.mult, ALU.add
                                        ).then_inc(var_ready, 1)

            def norm2_apply(b, c, powers, steps, t, last_half):
                if not last_half:
                    if t == 0:
                        dve.wait_ge(out_done, y_count(b, c) * 16)
                    last = nc.vector.scalar_tensor_tensor(out=y[:, t, :], in0=x[:, b, c * CT + t, :], scalar=mv2[:, t, 0:1],
                                                          in1=lng[:, :], op0=ALU.subtract, op1=ALU.mult)
                    if t == CT - 1:
                        last.then_inc(ln_step, 1)
                    return
                if t == 0:
                    dve.wait_ge(ln_step, steps + 3)
                    dve.wait_ge(rstd_ready, powers)
                    dve.wait_ge(x1b_ready, b * NC + (c + 1))
                last = nc.vector.scalar_tensor_tensor(out=y[:, t, :], in0=y[:, t, :], scalar=rstd2[:, t:t + 1],
                                                      in1=x1b[:, t, :], op0=ALU.mult, op1=ALU.add)
                if t == CT - 1:
                    last.then_inc(y_ready, 1)

            def low(name, n, nb):
                c = int(name[-1])
                kind = name.rstrip("0123456789")
                order = ["k0", "qa0", "k1", "qa1", "qb0", "qb1"]
                bank = sh_ps if n is not None else start_bank(name)
                done = sh_read if n is not None else start_sem(name)
                dve.wait_ge(sh_full, start_full(name) if n is None else sh_fills(n))
                dve.wait_ge(hi_ready, nb * len(order) + (order.index(name) + 1))
                s = slice(c * CH, (c + 1) * CH)
                if kind == "k":
                    nc.vector.tensor_tensor(k_lo[:, s], bank[0:NKV * DL, :], k_hi[:, s].bitcast(F), ALU.subtract
                                            ).then_inc(done, 1)
                else:
                    nc.vector.tensor_tensor(q_lo[:, s], bank[:, :], q_hi[:, s].bitcast(F), ALU.subtract
                                            ).then_inc(done, 1)

            dve.sem_inc(u_ready, U_AHEAD)
            dve.sem_inc(u_read, U_AHEAD)
            for g in range(NKV):
                nc.vector.memset(ks[g][KS:KM, :].bitcast(F), 1.0)
            nc.vector.memset(ones[:, :], 1.0)
            nc.vector.memset(minus_half[:, :], -0.5).then_inc(consts_ready, 1)
            for c in range(NC):
                dve.wait_ge(x0_in[c], 16)
                norm1_stats(0, range(c * CT, (c + 1) * CT), c + 1)
            for c in range(NC):
                dve.wait_ge(rstd_ready, c + 1)
                for t in range(c * CT, (c + 1) * CT):
                    norm1_apply(0, t)
            for name in USES_START:
                if name[0] in "kq":
                    low(name, None, 0)
                if name in STATS_AFTER:
                    bb = STATS_AFTER.index(name) + 1
                    dve.wait_ge(x_in[bb - 1], 16)
                    norm1_stats(bb, range(TT), NC + bb)
                if name == "wo":
                    for i in range(MX_C0):
                        maxima(0, i)
                    split_max(0, 0, 0)
            dve.wait_ge(rstd_ready, NORMS1)
            dve.wait_ge(ln_in, 2 * 16)

            def use(name, b, g, kind):
                n = use_no(b, g, kind, name)
                w = b * 2 + g
                if name[0] in "kq":
                    low(name, n, b + 1)
                if name[:2] == "sT":
                    reciprocals(n)
                if name == "rT0":
                    divide(w, g, 0, n)
                if name == "rT1":
                    divide(w - 1, 1 - g, 1, n)
                if name[0] == "f":
                    residual(b - int(name[1]) // 2, int(name[1]), n)

            def batch(b, kind):
                steps, powers = (2 * NORMS1, NORMS1) if kind == FIRST else (b * 6 + (2 * NORMS1 - 3), b * 2 + (NORMS1 - 1))
                for g in range(NKV):
                    w = b * 2 + g
                    wn = b * 2 + (g + 1)
                    no_m = kind == LAST and g == 1
                    for e in range(NE):
                        units = mx_beside(kind, g, e)
                        here = list(units)
                        names = USES_AT[kind][g][e]
                        for part in range(4):
                            if part == 1 and names[0]:
                                use(names[0], b, g, kind)
                            for _ in range(mx_share(units, part)):
                                ahead, n = units.pop(0)
                                maxima(wn if ahead else w, n)
                            if part == 3 and names[1]:
                                use(names[1], b, g, kind)
                            if g == 0 and e == APPLY0_END and kind != FIRST:
                                norm2_apply(b - 1, 0, powers, steps - 3, part, True)
                            if g == 0 and e in (APPLY1, APPLY1 + 1) and kind != FIRST:
                                norm2_apply(b - 1, 1, powers + 1, steps, part, e > APPLY1)
                            if g == 1 and e == APPLY0:
                                norm2_apply(b, 0, powers + 1, steps, part, False)
                            if g == 0 and kind != LAST and (e, part) in NORM1_AT:
                                norm1_apply(b + 1, NORM1_AT.index((e, part)))
                        if (0, NMX - 1) in here:
                            split_max(w, 1, start_full("m0"))
                        if (1, MX_C0 - 1) in here:
                            split_max(wn, 0, sh_fills(use_no(b, g, kind, "m1")))
                        if (1, NMX - 1) in here:
                            split_max(wn, 1, sh_fills(use_no(b, g, kind, "m0")))
                        if ("f3" if g == 0 else "f1") in USES_AT[kind][g][e]:
                            norm2_stats(steps)
                        if (g == 0 and e == APPLY1 + 1 and kind != FIRST) or (g == 1 and e == APPLY0):
                            steps, powers = steps + 3, powers + 1
                return steps, powers

            batch(0, FIRST)
            with dve.Fori(1, B - 1) as b:
                batch(b, MID)
            steps, powers = batch(B - 1, LAST)
            reciprocals(USES_ALL + 1)
            divide(2 * B - 1, 1, 1, USES_ALL + 2)
            for t in range(CT):
                norm2_apply(B - 1, 0, powers, steps - 3, t, True)
            residual(B - 1, 2, USES_ALL + 3)
            residual(B - 1, 3, USES_ALL + 4)
            norm2_stats(steps)
            for last_half in (False, True):
                for t in range(CT):
                    norm2_apply(B - 1, 1, powers + 1, steps, t, last_half)

        @block.gpsimd
        def _(pool):
            pool.sem_inc(pair_done, PAIRS_AHEAD)
            pool.sem_inc(y_ready, Y_AHEAD)
            pool.sem_inc(out_done, 16 * Y_AHEAD)
            nc.gpsimd.memset(ident[:, :], 0.0).then_inc(const_step, 1)
            nc.gpsimd.memset(maskb[:, :], 0.0).then_inc(const_step, 1)
            pool.wait_ge(const_step, 2)
            nc.gpsimd.affine_select(out=ident[:, :], in_=ident[:, :], compare_op=ALU.not_equal, fill=1.0, base=0,
                                    pattern=[[-1, P]], channel_multiplier=1).then_inc(const_step, 1)
            nc.gpsimd.affine_select(out=maskb[:, :], in_=maskb[:, :], compare_op=ALU.is_ge, fill=MASKED, base=0,
                                    pattern=[[-1, P]], channel_multiplier=1).then_inc(const_step, 1)
            pool.wait_ge(const_step, 4)
            nc.gpsimd.tensor_copy(identb[:, :], ident[:, :]).then_inc(consts_ready, 1)

            def rsqrt(out, in_, n, count):
                pool.wait_ge(var_ready, count)
                nc.gpsimd.tensor_tensor(out, in_, minus_half[:, 0:n], ALU.pow).then_inc(rstd_ready, 1)

            def diagonal(w, e):
                c, kt = TILES[e]
                off = first_query(c, kt)
                slot = e // 2 if e % 2 == 0 else 6 + (e // 2) % 2
                wait_apart(pool, (exp_done, w * NST + ST_END[e]))
                blk = pr[:, slot, :, off:off + P]
                nc.gpsimd.affine_select(out=blk, in_=blk, compare_op=ALU.is_ge, fill=0.0, base=0,
                                        pattern=[[0, HG], [1, P]], channel_multiplier=-1).then_inc(diag_done, 1)

            def pair(w, e, h0, h1):
                c, kt = TILES[e]
                off = first_query(c, kt)
                pool.wait_ge(pv_done, pv_count(w, e))
                if kt >= CT * c:
                    pool.wait_ge(diag_done, w * TT + (kt + 1))
                else:
                    pool.wait_ge(exp_done, w * NST + ST_END[e])
                even = pr[:, e // 2, h0:h1, off:CH]
                last = nc.gpsimd.tensor_tensor(even, even, pr[:, 6 + (e // 2) % 2, h0:h1, off:CH], ALU.add)
                if h1 == HG:
                    last.then_inc(pair_done, 1)

            def add_bias(b, c, reads):
                pool.wait_ge(sh_read, reads)
                pool.wait_ge(y_ready, y_count(b, c))
                nc.gpsimd.tensor_tensor(x1b[:, :, :], x[:, b, c * CT:(c + 1) * CT, :], lnb[:, None, :].to_broadcast([P, CT, D]), ALU.add
                                        ).then_inc(x1b_ready, 1)

            pool.wait_ge(consts_ready, 2)
            for c in range(NC):
                rsqrt(rstd1[:, 0, c * CT:(c + 1) * CT], var1[:, 0, c * CT:(c + 1) * CT], CT, c + 1)
            for bb in range(1, B):
                rsqrt(rstd1[:, bb, :], var1[:, bb, :], TT, NC + bb)
            pool.wait_ge(ln_in, 2 * 16)
            diagonal(0, 0)

            def batch(b, kind):
                powers = NORMS1 if kind == FIRST else b * 2 + (NORMS1 - 1)
                for g in range(NKV):
                    w = b * 2 + g
                    for e in range(1, NE):
                        for what, tile, *heads in POOL_AT.get(e, []):
                            if what == "add":
                                pair(w, tile, *heads)
                            elif tile < NE:
                                diagonal(w, tile)
                            elif not (kind == LAST and g == 1):
                                diagonal(b * 2 + (g + 1), 0)
                        if g == 0 and "f3" in USES_AT[kind][g][e]:
                            rsqrt(rstd2[:, :], var2[:, :], CT, powers + 1)
                            add_bias(b - 1, 1, use_no(b, g, kind, "f3") + 1)
                            powers = powers + 1
                    if g:
                        rsqrt(rstd2[:, :], var2[:, :], CT, powers + 1)
                        powers = powers + 1
                        add_bias(b, 0, use_no(b, g, kind, "f1") + 1)
                return powers

            batch(0, FIRST)
            with pool.Fori(1, B - 1) as b:
                batch(b, MID)
            powers = batch(B - 1, LAST)
            rsqrt(rstd2[:, :], var2[:, :], CT, powers + 1)
            add_bias(B - 1, 1, USES_ALL + len(USES_END))


def kernel(L0_attn_x, L0_attn_wq, L0_attn_wk_down, L0_attn_wv_down, L0_attn_wk_up, L0_attn_wv_up, L0_attn_wo,
           L0_ffn_ln_g, L0_ffn_ln_b, **unused):
    import numpy as np
    from concourse import bacc
    from concourse.bass_utils import run_bass_kernel_spmd

    nc = bacc.Bacc("TRN2", target_bir_lowering=False, num_devices=1)
    given = {"x": L0_attn_x, "wq": L0_attn_wq, "wk_down": L0_attn_wk_down, "wv_down": L0_attn_wv_down,
             "wk_up": L0_attn_wk_up, "wv_up": L0_attn_wv_up, "wo": L0_attn_wo,
             "ln_g": L0_ffn_ln_g, "ln_b": L0_ffn_ln_b}
    arrays, args = {}, []
    for name, a in given.items():
        a = np.ascontiguousarray(a)
        arrays[f"in_{name}"] = a
        args.append(nc.dram_tensor(f"in_{name}", a.shape, mybir.dt.from_np(a.dtype), kind="ExternalInput").ap())
    out = nc.dram_tensor("out_y", (B, T, D), mybir.dt.float32, kind="ExternalOutput").ap()
    program(nc, *args, out)
    result = run_bass_kernel_spmd(nc, [arrays], core_ids=[0])
    return result.results[0]["out_y"]
```
